# Optimizing a Trainium2 kernel written in Bass

```python
import numpy as np
import jax
import jax.numpy as jnp

def _softmax(x, axis=-1):
    return jax.nn.softmax(x, axis=axis)

def _gelu(x):
    return jax.nn.gelu(x, approximate=True)

def _silu(x):
    return jax.nn.silu(x)

def _sigmoid(x):
    return jax.nn.sigmoid(x)

def _layernorm(x, axis=-1, eps=1e-05):
    m = jnp.mean(x, axis=axis, keepdims=True)
    v = jnp.var(x, axis=axis, keepdims=True)
    return (x - m) / jnp.sqrt(v + eps)

def _scatter_add(tgt, idx, src, axis=0):
    return tgt.at[idx].add(src)

def _segment_sum(src, seg, n):
    return jax.ops.segment_sum(src, seg, n)
kernel_name = 'mk_adaln_ffn_d1_seqx_r4_1da545'

def setup_inputs(seed: int=0):
    np.random.seed(seed)
    _w = jnp.asarray

    def _rec_inputs():
        import jax
        import jax.numpy as jnp
        _rk = jax.random.key(seed)
        x = -0.000125 + 0.9999 * jax.random.normal(jax.random.fold_in(_rk, 1), (32, 64, 1024), jnp.float32)
        _lenS = 64 - jax.random.randint(jax.random.fold_in(_rk, 7), (32,), 0, max(1, 64 // 4) + 1, jnp.int32)
        _lenS2 = 64 - jax.random.randint(jax.random.fold_in(_rk, 8), (32,), 0, max(1, 64 // 4) + 1, jnp.int32)
        cond_128 = 0.0061147 + 1.02565 * jax.random.normal(jax.random.fold_in(_rk, 11), (32, 128), jnp.float32)
        fside_S_0 = -0.022604 + 0.987366 * jax.random.normal(jax.random.fold_in(_rk, 12), (64,), jnp.float32)
        return (x, cond_128, fside_S_0)
    x, cond_128, fside_S_0 = _rec_inputs()

    def _L0_cond_setup():
        import jax, jax.numpy as jnp
        import numpy as np
        from jax import lax
        N, C_IN, L = (32, 64, 1024)
        C_OUT, K, GROUPS = (64, 9, 4)
        C_DIM, PAD, STRIDE = (128, 4, 1)
        key = jax.random.key(seed)
        k1, k2, k3, k4, k5 = jax.random.split(key, 5)
        x = jax.random.normal(k1, (N, C_IN, L), dtype=jnp.float32)
        c = jax.random.normal(k2, (N, C_DIM), dtype=jnp.float32)
        weight = jax.random.normal(k3, (C_OUT, C_IN // GROUPS, K), dtype=jnp.float32)
        c_weight = jax.random.normal(k4, (C_OUT, C_DIM), dtype=jnp.float32)
        bias = jax.random.normal(k5, (C_OUT,), dtype=jnp.float32)
        return {'x': x, 'c': c, 'weight': weight, 'c_weight': c_weight, 'bias': bias}
    _L0_cond_all = _L0_cond_setup()
    _L0_cond_in = {k: v for k, v in _L0_cond_all.items() if k in ('weight', 'c_weight')}
    del _L0_cond_all

    def _L0_ffn_setup():
        import jax, jax.numpy as jnp
        import numpy as np
        N_STREAMS = 4
        DIM = 256
        SINKHORN_ITERS = 50
        SINKHORN_TAU = 0.1
        RMS_EPS = 1.1920929e-07

        def sinkhorn_log(logits, num_iters=SINKHORN_ITERS, tau=SINKHORN_TAU):
            Z = logits / tau
            u0 = jnp.zeros(Z.shape[:-1], Z.dtype)
            v0 = jnp.zeros_like(u0)

            def step(carry, _):
                u, v = carry
                u = -jax.nn.logsumexp(Z + v[..., None, :], axis=-1)
                v = -jax.nn.logsumexp(Z + u[..., :, None], axis=-2)
                return ((u, v), None)
            (u, v), _ = jax.lax.scan(step, (u0, v0), None, length=num_iters)
            return jnp.exp(Z + u[..., :, None] + v[..., None, :])
        key = jax.random.key(seed)
        ks = jax.random.split(key, 6)
        B, T = (4, 512)
        n, C = (N_STREAMS, DIM)
        wd = n * C
        x = jax.random.normal(ks[0], (B, T, wd), dtype=jnp.float32)
        W_res = 0.01 * jax.random.normal(ks[1], (n * n, wd), dtype=jnp.float32)
        W_pre = 0.01 * jax.random.normal(ks[2], (n, wd), dtype=jnp.float32)
        W_post = 0.01 * jax.random.normal(ks[3], (n, wd), dtype=jnp.float32)
        H_res_base = jnp.full((n, n), -0.5, dtype=jnp.float32)
        H_res_base = H_res_base.at[jnp.arange(n), jnp.arange(n)].set(0.0)
        H_pre_base = jnp.zeros((n,), dtype=jnp.float32).at[0].set(1.0)
        H_post_base = jnp.zeros((n,), dtype=jnp.float32)
        gate = jnp.array([5.0], dtype=jnp.float32)
        W_branch = 1.0 / np.sqrt(C) * jax.random.normal(ks[4], (C, C), dtype=jnp.float32)
        return {'x': x, 'W_res': W_res, 'W_pre': W_pre, 'W_post': W_post, 'H_res_base': H_res_base, 'H_pre_base': H_pre_base, 'H_post_base': H_post_base, 'gate': gate, 'W_branch': W_branch}
    _L0_ffn_all = _L0_ffn_setup()
    _L0_ffn_in = {k: v for k, v in _L0_ffn_all.items() if k in ('W_res', 'W_pre', 'W_post', 'H_res_base', 'H_pre_base', 'H_post_base', 'gate', 'W_branch')}
    del _L0_ffn_all
    return {'x': x, 'cond_128': cond_128, 'fside_S_0': fside_S_0, 'L0_cond_weight': _L0_cond_in['weight'], 'L0_cond_c_weight': _L0_cond_in['c_weight'], 'L0_ffn_W_res': _L0_ffn_in['W_res'], 'L0_ffn_W_pre': _L0_ffn_in['W_pre'], 'L0_ffn_W_post': _L0_ffn_in['W_post'], 'L0_ffn_H_res_base': _L0_ffn_in['H_res_base'], 'L0_ffn_H_pre_base': _L0_ffn_in['H_pre_base'], 'L0_ffn_H_post_base': _L0_ffn_in['H_post_base'], 'L0_ffn_gate': _L0_ffn_in['gate'], 'L0_ffn_W_branch': _L0_ffn_in['W_branch']}

def reference(x, cond_128, fside_S_0, L0_cond_weight, L0_cond_c_weight, L0_ffn_W_res, L0_ffn_W_pre, L0_ffn_W_post, L0_ffn_H_res_base, L0_ffn_H_pre_base, L0_ffn_H_post_base, L0_ffn_gate, L0_ffn_W_branch):
    import jax
    import jax.numpy as jnp

    def _L0_cond_ref(x, c, weight, c_weight, bias):
        import jax, jax.numpy as jnp
        import numpy as np
        from jax import lax
        N, C_IN, L = (32, 64, 1024)
        C_OUT, K, GROUPS = (64, 9, 4)
        C_DIM, PAD, STRIDE = (128, 4, 1)
        out = lax.conv_general_dilated(x, weight, window_strides=(STRIDE,), padding=[(PAD, PAD)], dimension_numbers=('NCH', 'OIH', 'NCH'), feature_group_count=GROUPS)
        ctx = jnp.einsum('nd,od->no', c, c_weight)
        out = out + ctx[:, :, None] + bias[None, :, None]
        return out

    def _L0_ffn_ref(x, W_res, W_pre, W_post, H_res_base, H_pre_base, H_post_base, gate, W_branch):
        import jax, jax.numpy as jnp
        import numpy as np
        N_STREAMS = 4
        DIM = 256
        SINKHORN_ITERS = 50
        SINKHORN_TAU = 0.1
        RMS_EPS = 1.1920929e-07

        def sinkhorn_log(logits, num_iters=SINKHORN_ITERS, tau=SINKHORN_TAU):
            Z = logits / tau
            u0 = jnp.zeros(Z.shape[:-1], Z.dtype)
            v0 = jnp.zeros_like(u0)

            def step(carry, _):
                u, v = carry
                u = -jax.nn.logsumexp(Z + v[..., None, :], axis=-1)
                v = -jax.nn.logsumexp(Z + u[..., :, None], axis=-2)
                return ((u, v), None)
            (u, v), _ = jax.lax.scan(step, (u0, v0), None, length=num_iters)
            return jnp.exp(Z + u[..., :, None] + v[..., None, :])
        B, T, nC = x.shape
        n = N_STREAMS
        C = nC // n
        x_norm = x * jax.lax.rsqrt(jnp.mean(x * x, axis=-1, keepdims=True) + RMS_EPS)
        H_res_logits = (x_norm @ W_res.T).reshape(B, T, n, n) + H_res_base
        H_pre_logits = x_norm @ W_pre.T + H_pre_base
        H_post_logits = x_norm @ W_post.T + H_post_base
        H_res = sinkhorn_log(H_res_logits)
        H_pre = jax.nn.softmax(H_pre_logits, axis=-1)
        H_post = jax.nn.softmax(H_post_logits, axis=-1)
        g = jax.nn.sigmoid(gate)[0]
        I = jnp.eye(n, dtype=H_res.dtype)
        H_res = (1.0 - g) * I + g * H_res
        x_streams = x.reshape(B, T, n, C)
        x_pre = jnp.einsum('btnc,btn->btc', x_streams, H_pre)
        y = x_pre @ W_branch
        x_mixed = jnp.einsum('btij,btjc->btic', H_res, x_streams)
        y_distributed = jnp.einsum('btc,btn->btnc', y, H_post)
        return (x_mixed + y_distributed).reshape(B, T, nC)
    x = x + _L0_ffn_ref(_L0_cond_ref(x, cond_128, L0_cond_weight, L0_cond_c_weight, fside_S_0), L0_ffn_W_res, L0_ffn_W_pre, L0_ffn_W_post, L0_ffn_H_res_base, L0_ffn_H_pre_base, L0_ffn_H_post_base, L0_ffn_gate, L0_ffn_W_branch)
    return x

_drawn_inputs = setup_inputs


def setup_inputs(seed=0):
    import zlib

    import numpy as np

    out = dict(_drawn_inputs(seed))
    spreads = {'L0_ffn_H_post_base': (0.0, 0.592)}
    factors = {}
    for name, (base, spread) in spreads.items():
        noise = np.random.default_rng([zlib.crc32(name.encode()), seed]).standard_normal(out[name].shape)
        drawn = base * np.exp(spread * noise) if base else spread * noise
        out[name] = jnp.asarray(drawn.astype(out[name].dtype))
    for name, factor in factors.items():
        out[name] = (out[name] * factor).astype(out[name].dtype)
    return out
```

```python
import numpy as np


def adaln_ffn_program(nc, x, out, conv_w, ctx_w, cond_t, bias_c, proj_w, branch_w, base, gate, consts):
    import concourse.bass as bass
    from concourse import mybir
    from contextlib import ExitStack

    f32 = mybir.dt.float32
    ALU = mybir.AluOpType
    ACT = mybir.ActivationFunctionType
    AX = mybir.AxisListType
    ds = bass.ds

    N, CH, L = x.shape
    P = 128
    BT = 32
    NS = 4
    C = L // NS
    NBLK = N * CH // BT
    UB = 4
    NU = NBLK // UB
    QU = 4
    NQ = NU // QU
    CU = 8
    NCH = NU // CU
    TS, TQ = 3, 3
    PAD = 4
    XW = L + 2 * PAD - TS + 1
    NE = NS * NS + 2 * NS
    HH = NS * NS
    SINK_ITERS = 50
    TAU_INV = 10.0
    RMS_EPS = 1.1920929e-07
    BIG = float(2.0 ** 120)
    LN_BIG = float(120.0 * np.log(2.0))
    CLAMP = -8.0

    with ExitStack() as ctx:
        def sb(name, shape):
            return ctx.enter_context(nc.sbuf_tensor(name, shape, f32))

        def pb(name):
            return ctx.enter_context(nc.psum_tensor(name, [P, 512], f32))

        def sem(name):
            return ctx.enter_context(nc.semaphore(name))

        cst = sb("cst", [P, 2 * P + 8 + NE + HH])
        ident = cst[:, 0:P]
        tok4 = cst[:, P:2 * P]
        bmask = cst[:, 2 * P:2 * P + 4]
        select = cst[:, 2 * P + 8:2 * P + 8 + NE]
        eye4 = cst[:, 2 * P + 8 + NE:2 * P + 8 + NE + HH]
        convw = sb("convw", [TS * BT, 2, TQ, BT])
        projw = sb("projw", [P, 2, NS, BT])
        branchw = sb("branchw", [P, 2, C])
        ctxw = sb("ctxw", [P, 2, P])
        condt = sb("condt", [P, N])
        biasc = sb("biasc", [P, 2])
        base_s = sb("base_s", [P, NE])
        gate_s = sb("gate_s", [P, 1])
        bias_all = sb("bias_all", [P, NBLK])
        g_s = sb("g_s", [P, 4])
        g_eye = sb("g_eye", [P, HH])
        lnbig = sb("lnbig", [P, 1])

        xin = sb("xin", [TS * BT, QU, UB, XW])
        h_now = sb("h_now", [P, 2, UB, C])
        h_all = sb("h_all", [P, NBLK, C])
        ht_y = sb("ht_y", [P, 2 * QU * 512])
        ht = ht_y[:, :].rearrange("p (a k n) -> p a k n", a=2, k=QU)
        y_all = ht_y[:, :].rearrange("p (u c) -> p u c", u=NU)
        sq_junk = sb("sq_junk", [P, 2, C])
        ssq = sb("ssq", [P, NBLK])
        lp_s = sb("lp_s", [P, 512])
        raw_l = sb("raw_l", [P, NU, NE])
        raw_s = sb("raw_s", [P, NU, UB])

        t_s = sb("t_s", [P, CU, UB])
        ss = sb("ss", [P, CU])
        ms = sb("ms", [P, CU])
        rt = sb("rt", [P, CU])
        inv = sb("inv", [P, CU])
        lg = sb("lg", [P, CU, NE])
        la = sb("la", [P, CU, NE])
        gmax = sb("gmax", [P, CU * NE // NS])
        colmax = sb("colmax", [P, CU, NS])
        zb = sb("zb", [P, NS, CU, NS])
        zc = sb("zc", [P, NS, CU, NS])
        e_h = sb("e_h", [P, CU, HH])
        e_p = sb("e_p", [P, CU, 2 * NS])
        p_a = sb("p_a", [P, NS, CU, NS])
        p_b = sb("p_b", [P, NS, CU, NS])
        s_a = sb("s_a", [P, NS, CU])
        r_a = sb("r_a", [P, NS, CU])
        s_p = sb("s_p", [P, 2 * CU])
        r_p = sb("r_p", [P, 2 * CU])
        soft = sb("soft", [P, NU, 2 * NS])
        sk = sb("sk", [P, NS, CU, NS])
        sk_s = sb("sk_s", [P, NS * CU])
        sk_r = sb("sk_r", [P, NS * CU])
        hk = sb("hk", [P, CU, HH])
        mv_h = sb("mv_h", [P, CU, UB, HH])
        mv_p = sb("mv_p", [P, NU, UB, NS])
        xf_h = sb("xf_h", [P, CU * UB * NS, NS])
        xf_p = sb("xf_p", [P, NBLK, NS])
        coef = sb("coef", [P, NBLK, NS])
        coef_p = sb("coef_p", [P, NBLK])

        pre_m = sb("pre_m", [P, 2, UB, BT])
        res_m = sb("res_m", [P, 2, UB, NS, BT])
        post_m = sb("post_m", [P, 2, UB, NS, BT])
        xp_s = sb("xp_s", [P, 2, C])
        xpt_s = sb("xpt_s", [P, 2, C])
        xres = sb("xres", [P, 2, UB, C])
        ost = h_now

        banks = [pb(f"bank{i}") for i in range(8)]
        conv_ps = [banks[0], banks[1]]
        ht_ps = [banks[2], banks[3]]
        lp_ps = banks[4]
        sel_ps = banks[5]
        xp_ps, xpt_ps, y_ps = banks[2], banks[3], banks[4]
        mix_ps = [[banks[0], banks[1]], [banks[6], banks[7]]]
        xfh_ps, xfp_ps = banks[5], banks[6]

        w_loaded = sem("w_loaded")
        x_margin = sem("x_margin")
        x_loaded = [sem(f"x_loaded{k}") for k in range(QU)]
        conv_done = sem("conv_done")
        h_ready = sem("h_ready")
        conv_read = sem("conv_read")
        h_kept = sem("h_kept")
        t_done = sem("t_done")
        ht_ready = sem("ht_ready")
        logit_done = sem("logit_done")
        lp_ready = sem("lp_ready")
        sel_done = sem("sel_done")
        raw_ready = sem("raw_ready")
        ctx_done = sem("ctx_done")
        bias_ready = sem("bias_ready")
        gexp = sem("gexp")
        dve = sem("dve")
        ms_ready = sem("ms_ready")
        rt_ready = sem("rt_ready")
        args_ready = sem("args_ready")
        exps_ready = sem("exps_ready")
        mvp_ready = sem("mvp_ready")
        mvh_ready = sem("mvh_ready")
        xfp_done = sem("xfp_done")
        xfh_done = sem("xfh_done")
        pre_ready = sem("pre_ready")
        coef_ready = sem("coef_ready")
        pre_built = sem("pre_built")
        xp_done = sem("xp_done")
        xp_ready = sem("xp_ready")
        xpt_done = sem("xpt_done")
        xpt_ready = sem("xpt_ready")
        y_done = sem("y_done")
        y_ready = sem("y_ready")
        mix_built = sem("mix_built")
        mix_done = sem("mix_done")
        mix_read = [sem("mix_read_act"), sem("mix_read_dve")]
        sum_ready = [sem("sum_ready_pool"), sem("sum_ready_dve")]
        r_loaded = [sem(f"r_loaded{k}") for k in range(2)]
        stored = [sem(f"stored{k}") for k in range(2)]

        W_LOADS = 9

        x_cv = x.rearrange("n (h c) l -> c (n h) l", h=2)
        x_tok = x.rearrange("n (h c) (j l) -> j c (n h) l", h=2, j=NS)
        o_tok = out.rearrange("n (h c) (j l) -> j c (n h) l", h=2, j=NS)

        block = ctx.enter_context(nc.Block())

        @block.sync
        def _(sp):
            def load_unit(u, k):
                for s in range(TS):
                    sp.dma_start(xin[BT * s:BT * (s + 1), k, :, PAD - s:PAD - s + L],
                                 x_cv[:, ds(UB * u, UB), :]).then_inc(x_loaded[k], 16)

            def load_res(u, slot):
                for j in range(NS):
                    sp.dma_start(xres[BT * j:BT * (j + 1), slot, :, :],
                                 x_tok[j, :, ds(UB * u, UB), :]).then_inc(r_loaded[slot], 16)

            def store(u, c, slot):
                sp.wait_ge(sum_ready[c], u - CU * c + 1)
                for j in range(NS):
                    sp.dma_start(o_tok[j, :, ds(UB * u, UB), :],
                                 ost[BT * j:BT * (j + 1), slot, :, :]).then_inc(stored[slot], 16)

            sp.dma_start(convw[:], conv_w).then_inc(w_loaded, 16)
            sp.wait_ge(x_margin, 1)
            load_unit(0, 0)
            for dst, src in ((ctxw, ctx_w), (condt, cond_t), (biasc, bias_c), (cst, consts), (projw, proj_w),
                             (branchw, branch_w), (base_s, base), (gate_s, gate)):
                sp.dma_start(dst[:], src).then_inc(w_loaded, 16)
            for k in range(1, QU):
                load_unit(k, k)
            with sp.Fori(1, NQ) as i:
                for k in range(QU):
                    sp.wait_ge(conv_done, 2 * QU * i + 2 * (k + 1 - QU))
                    load_unit(QU * i + k, k)
            for slot in range(2):
                load_res(slot, slot)
            with sp.Fori(0, CU // 2) as i:
                for slot in range(2):
                    store(2 * i + slot, 0, slot)
                    load_res(2 * i + slot + 2, slot)
            with sp.Fori(CU // 2, NU // 2 - 1) as i:
                for slot in range(2):
                    store(2 * i + slot, 1, slot)
                    load_res(2 * i + slot + 2, slot)
            for slot in range(2):
                store(NU - 2 + slot, 1, slot)
            for slot in range(2):
                sp.wait_ge(stored[slot], 16 * NS * NU // 2)

        @block.tensor
        def _(pe):
            def conv(u, k, i, half, first=False):
                if half == 0:
                    pe.wait_ge(x_loaded[k], 16 * TS * (i + 1))
                if not first:
                    pe.wait_ge(conv_read, 2 * u + half - 1)
                for q in range(TQ):
                    for j in range(NS):
                        last = nc.tensor.matmul(conv_ps[half][BT * j:BT * (j + 1), :].rearrange("p (b c) -> p b c", b=2),
                                                convw[:, half, q, :],
                                                xin[:, k, half::2, C * j + TS * q:C * j + TS * q + C],
                                                start=(q == 0), stop=(q == TQ - 1))
                last.then_inc(conv_done, 1)

            def transpose_h(u, slot, first=False):
                pe.wait_ge(h_ready, 2 * u + 2)
                for a in range(2):
                    if not first:
                        pe.wait_ge(ht_ready, 2 * u + a - 1)
                    for b in range(UB):
                        last = nc.tensor.transpose(ht_ps[a][:, P * b:P * (b + 1)],
                                                   h_now[:, slot, b, P * a:P * (a + 1)], ident)
                    last.then_inc(t_done, 1)

            def logits(i):
                pe.wait_ge(ht_ready, 2 * QU * (i + 1))
                for a in range(2):
                    hv = ht[:, a].rearrange("p k (b j t) -> p (k b) j t", b=UB, j=NS)
                    for j in range(NS):
                        last = nc.tensor.matmul(lp_ps[BT * j:BT * (j + 1), :], projw[:, a, j, :], hv[:, :, j, :],
                                                start=(a == 0), stop=(a == 1))
                last.then_inc(logit_done, 1)

            def to_tokens(i):
                pe.wait_ge(lp_ready, i + 1)
                pe.wait_ge(raw_ready, i)
                for k in range(QU):
                    nc.tensor.matmul(sel_ps[:, NE * k:NE * (k + 1)], lp_s[:, P * k:P * (k + 1)], select,
                                     start=True, stop=True)
                nc.tensor.matmul(sel_ps[:, NE * QU:NE * QU + UB * QU], tok4, ssq[:, ds(UB * QU * i, UB * QU)],
                                 start=True, stop=True).then_inc(sel_done, 1)

            def quad(i, first):
                u = QU * i
                conv(u, 0, i, 0, first=first)
                if not first:
                    transpose_h(u - 1, 1)
                conv(u, 0, i, 1, first=first)
                if not first:
                    logits(i - 1)
                conv(u + 1, 1, i, 0)
                if not first:
                    to_tokens(i - 1)
                conv(u + 1, 1, i, 1)
                transpose_h(u, 0, first=first)
                for k in (2, 3):
                    conv(u + k, k, i, 0)
                    conv(u + k, k, i, 1)
                    transpose_h(u + k - 1, (k - 1) % 2)

            def x_pre(u, slot, first=False):
                pe.wait_ge(pre_built, u + 1)
                if not first:
                    pe.wait_ge(xp_ready, u)
                for b in range(UB):
                    last = nc.tensor.matmul(xp_ps[BT * b:BT * (b + 1), 0:C], pre_m[:, slot, b, :],
                                            h_all[:, UB * u + b, :], start=True, stop=True)
                last.then_inc(xp_done, 1)

            def x_pre_t(u, slot, first=False):
                pe.wait_ge(xp_ready, u + 1)
                if not first:
                    pe.wait_ge(xpt_ready, u)
                for a in range(2):
                    last = nc.tensor.transpose(xpt_ps[:, P * a:P * (a + 1)],
                                               xp_s[:, slot, P * a:P * (a + 1)], ident)
                last.then_inc(xpt_done, 1)

            def branch(u, slot, first=False):
                pe.wait_ge(xpt_ready, u + 1)
                if not first:
                    pe.wait_ge(y_ready, u)
                for a in range(2):
                    last = nc.tensor.matmul(y_ps[:, 0:C], xpt_s[:, slot, P * a:P * (a + 1)],
                                            branchw[:, a, :], start=(a == 0), stop=(a == 1))
                last.then_inc(y_done, 1)

            def branch_chunk(c):
                for t in range(CU * c, CU * (c + 1) + 2):
                    if t < CU * (c + 1):
                        x_pre(t, t % 2, t == 0)
                    if CU * c <= t - 1 < CU * (c + 1):
                        x_pre_t(t - 1, (t - 1) % 2, t - 1 == 0)
                    if t - 2 >= CU * c:
                        branch(t - 2, t % 2, t - 2 == 0)

            def mix(u, c, slot, prev):
                pe.wait_ge(mix_built, u + 1)
                pe.wait_ge(y_ready, u + 1)
                for bp in range(2):
                    if prev is not None:
                        pe.wait_ge(mix_read[prev], 2 * (u - CU * prev) + bp - 3)
                    for b in (2 * bp, 2 * bp + 1):
                        o = mix_ps[slot][bp][:, C * (b % 2):C * (b % 2 + 1)]
                        nc.tensor.matmul(o, res_m[:, slot, b], h_all[:, ds(UB * u + b, 1), :], start=True, stop=False)
                        last = nc.tensor.matmul(o, post_m[:, slot, b], y_all[:, ds(u, 1), :], start=False, stop=True)
                    last.then_inc(mix_done, 1)

            def mix_chunk(c):
                u = CU * c
                for slot in range(2):
                    mix(u + slot, c, slot, c - 1 if c else None)
                with pe.Fori(u // 2 + 1, (u + CU) // 2) as i:
                    for slot in range(2):
                        mix(2 * i + slot, c, slot, c)

            def spread_res(c):
                pe.wait_ge(mvh_ready, c + 1)
                nc.tensor.matmul(xfh_ps[:, :], tok4, mv_h[:].rearrange("p u b e -> p (u b e)"),
                                 start=True, stop=True).then_inc(xfh_done, 1)

            pe.wait_ge(w_loaded, 16 * W_LOADS)
            for half in range(2):
                last = nc.tensor.matmul(sel_ps[:, N * half:N * (half + 1)], ctxw[:, half, :], condt[:],
                                        start=True, stop=True)
            last.then_inc(ctx_done, 1)
            quad(0, True)
            with pe.Fori(1, NQ) as i:
                quad(i, False)
            transpose_h(NU - 1, 1)
            logits(NQ - 1)
            to_tokens(NQ - 1)
            pe.wait_ge(mvp_ready, 1)
            nc.tensor.matmul(xfp_ps[:, 0:NBLK * NS], tok4, mv_p[:].rearrange("p u b e -> p (u b e)"),
                             start=True, stop=True).then_inc(xfp_done, 1)
            spread_res(0)
            branch_chunk(0)
            mix_chunk(0)
            branch_chunk(1)
            spread_res(1)
            mix_chunk(1)

        @block.scalar
        def _(act):
            def conv_out(u, slot, half, first=False):
                if half == 0 and not first:
                    act.wait_ge(t_done, 2 * u - 2)
                    act.wait_ge(h_kept, u - 1)
                act.wait_ge(conv_done, 2 * u + half + 1)
                for n in range(2):
                    b = 2 * n + half
                    last = nc.scalar.activation(h_now[:, slot, b, :], conv_ps[half][:, C * n:C * (n + 1)], ACT.Identity,
                                                bias=bias_all[:, ds(UB * u + b, 1)])
                last.then_inc(h_ready, 1)
                act.wait_ge(conv_read, 2 * u + half)
                for n in range(2):
                    b = UB * u + 2 * n + half
                    last = nc.scalar.activation(sq_junk[:, n, :], conv_ps[half][:, C * n:C * (n + 1)], ACT.Square,
                                                bias=bias_all[:, ds(b, 1)], accum_out=ssq[:, ds(b, 1)])
                last.then_inc(conv_read, 1)

            def ht_out(u, k, i):
                for a in range(2):
                    act.wait_ge(t_done, 2 * u + a + 1)
                    if i:
                        act.wait_ge(logit_done, i)
                    nc.scalar.copy(ht[:, a, k, :], ht_ps[a][:, :]).then_inc(ht_ready, 1)

            def logits_out(i):
                act.wait_ge(logit_done, i + 1)
                if i:
                    act.wait_ge(sel_done, i)
                nc.scalar.copy(lp_s[:], lp_ps[:, :]).then_inc(lp_ready, 1)

            def tokens_out(i):
                act.wait_ge(sel_done, i + 1)
                nc.scalar.copy(raw_l[:, QU * i:QU * (i + 1), :],
                               sel_ps[:, 0:NE * QU].rearrange("p (k e) -> p k e", e=NE))
                nc.scalar.copy(raw_s[:, QU * i:QU * (i + 1), :],
                               sel_ps[:, NE * QU:(NE + UB) * QU].rearrange("p (k e) -> p k e", e=UB)).then_inc(raw_ready, 1)

            def root(c):
                act.wait_ge(ms_ready, c + 1)
                nc.scalar.activation(rt[:], ms[:], ACT.Sqrt).then_inc(rt_ready, 1)

            def exponentials(c):
                act.wait_ge(args_ready, c + 1)
                nc.scalar.activation(e_h[:], la[:, :, 0:HH], ACT.Exp, scale=TAU_INV)
                nc.scalar.activation(e_p[:], la[:, :, HH:NE], ACT.Exp)
                nc.scalar.activation(p_a[:], zb[:], ACT.Exp, scale=TAU_INV)
                nc.scalar.activation(p_b[:], zc[:], ACT.Exp, scale=TAU_INV, bias=lnbig[:, 0:1]).then_inc(exps_ready, 1)

            def quad(i):
                u = QU * i
                conv_out(u, 0, 0, i == 0)
                if i:
                    ht_out(u - 1, 3, i - 1)
                conv_out(u, 0, 1, i == 0)
                if i:
                    logits_out(i - 1)
                conv_out(u + 1, 1, 0, i == 0)
                if i:
                    tokens_out(i - 1)
                conv_out(u + 1, 1, 1)
                if i == 2:
                    root(0)
                ht_out(u, 0, i)
                conv_out(u + 2, 0, 0)
                conv_out(u + 2, 0, 1)
                if i == 2:
                    exponentials(0)
                ht_out(u + 1, 1, i)
                conv_out(u + 3, 1, 0)
                conv_out(u + 3, 1, 1)
                ht_out(u + 2, 2, i)

            def x_pre_out(u, slot, first=False):
                act.wait_ge(xp_done, u + 1)
                if not first:
                    act.wait_ge(xpt_done, u - 1)
                nc.scalar.copy(xp_s[:, slot, :], xp_ps[:, 0:C]).then_inc(xp_ready, 1)

            def x_pre_t_out(u, slot, first=False):
                act.wait_ge(xpt_done, u + 1)
                if not first:
                    act.wait_ge(y_done, u - 1)
                nc.scalar.copy(xpt_s[:, slot, :], xpt_ps[:, 0:C]).then_inc(xpt_ready, 1)

            def branch_out(u, slot):
                act.wait_ge(y_done, u + 1)
                nc.scalar.copy(y_all[:, ds(u, 1), :], y_ps[:, 0:C]).then_inc(y_ready, 1)

            def branch_chunk(c):
                u = CU * c
                x_pre_out(u, 0, c == 0)
                x_pre_out(u + 1, 1, c == 0)
                x_pre_t_out(u, 0, c == 0)
                if c == 0:
                    x_pre_out(2, 0)
                    x_pre_t_out(1, 1, True)
                    branch_out(0, 0)
                    x_pre_out(3, 1)
                    x_pre_t_out(2, 0)
                    branch_out(1, 1)
                with act.Fori(u // 2 + (2 if c == 0 else 1), (u + CU) // 2) as i:
                    for slot in range(2):
                        x_pre_out(2 * i + slot, slot)
                        x_pre_t_out(2 * i + slot - 1, 1 - slot)
                        branch_out(2 * i + slot - 2, slot)
                x_pre_t_out(u + CU - 1, 1)
                branch_out(u + CU - 2, 0)
                branch_out(u + CU - 1, 1)

            act.wait_ge(w_loaded, 16 * W_LOADS)
            nc.scalar.activation(g_s[:, 0:1], gate_s[:], ACT.Exp, scale=-1.0).then_inc(gexp, 1)
            act.wait_ge(bias_ready, 1)
            for i in range(NQ):
                quad(i)
            ht_out(NU - 1, 3, NQ - 1)
            logits_out(NQ - 1)
            tokens_out(NQ - 1)
            root(1)
            exponentials(1)
            branch_chunk(0)

            def mix_out(u, slot):
                for bp in range(2):
                    act.wait_ge(mix_done, 2 * u + bp + 1)
                    nc.scalar.copy(ost[:, slot, 2 * bp:2 * bp + 2, :],
                                   mix_ps[slot][bp][:, :].rearrange("p (b c) -> p b c", b=2)).then_inc(mix_read[0], 1)

            act.wait_ge(h_kept, NU)
            for slot in range(2):
                mix_out(slot, slot)
            with act.Fori(1, CU // 2) as i:
                for slot in range(2):
                    act.wait_ge(stored[slot], 16 * NS * i)
                    mix_out(2 * i + slot, slot)
            branch_chunk(1)

        @block.gpsimd
        def _(pool):
            nc.gpsimd.memset(xin[:, :, :, 0:PAD], 0.0)
            nc.gpsimd.memset(xin[:, :, :, XW - PAD:XW], 0.0).then_inc(x_margin, 1)
            nc.gpsimd.memset(lnbig[:], LN_BIG).then_inc(x_margin, 1)

            with pool.Fori(0, NU // 2) as i:
                for slot in range(2):
                    pool.wait_ge(h_ready, 4 * i + 2 * slot + 2)
                    nc.gpsimd.tensor_copy(h_all[:, ds(UB * (2 * i + slot), UB), :], h_now[:, slot]).then_inc(h_kept, 1)

            lane = tok4[:, 0:BT]

            def build_pre(u, slot, first=False):
                if not first:
                    pool.wait_ge(xp_done, u - 1)
                nc.gpsimd.tensor_tensor(pre_m[:, slot], lane.unsqueeze(1).to_broadcast([P, UB, BT]),
                                        coef_p[:, ds(UB * u, UB)].unsqueeze(2).to_broadcast([P, UB, BT]),
                                        ALU.mult).then_inc(pre_built, 1)

            def build_mix(u, slot, first=False):
                if not first:
                    pool.wait_ge(mix_done, 2 * u - 2)
                nc.gpsimd.tensor_tensor(
                    res_m[:, slot].rearrange("p b i t -> p (b i) t"),
                    lane.unsqueeze(1).to_broadcast([P, UB * NS, BT]),
                    coef[:, ds(UB * u, UB), :].rearrange("p b i -> p (b i)").unsqueeze(2).to_broadcast([P, UB * NS, BT]),
                    ALU.mult)
                nc.gpsimd.tensor_tensor(
                    post_m[:, slot],
                    ident.rearrange("p (b t) -> p b t", b=UB).unsqueeze(2).to_broadcast([P, UB, NS, BT]),
                    soft[:, ds(u, 1), NS:2 * NS].rearrange("p u i -> p (u i)").unsqueeze(1).unsqueeze(3)
                    .to_broadcast([P, UB, NS, BT]),
                    ALU.mult).then_inc(mix_built, 1)

            def add_res(u, slot):
                pool.wait_ge(mix_read[0], 2 * u + 2)
                pool.wait_ge(r_loaded[slot], 16 * NS * (u // 2 + 1) if isinstance(u, int) else 8 * NS * (u - slot) + 16 * NS)
                nc.gpsimd.tensor_tensor(ost[:, slot], ost[:, slot], xres[:, slot], ALU.add).then_inc(sum_ready[0], 1)

            pool.wait_ge(pre_ready, 1)
            for slot in range(2):
                build_pre(slot, slot, True)
            with pool.Fori(1, CU // 2) as i:
                for slot in range(2):
                    build_pre(2 * i + slot, slot)
            pool.wait_ge(coef_ready, 1)
            for slot in range(2):
                build_mix(slot, slot, True)
            with pool.Fori(0, CU // 2 - 1) as i:
                for slot in range(2):
                    add_res(2 * i + slot, slot)
                    build_mix(2 * i + slot + 2, slot)
            for slot in range(2):
                add_res(CU - 2 + slot, slot)
            with pool.Fori(CU // 2, NU // 2) as i:
                for slot in range(2):
                    build_pre(2 * i + slot, slot)
            pool.wait_ge(coef_ready, 2)
            with pool.Fori(CU // 2, NU // 2) as i:
                for slot in range(2):
                    build_mix(2 * i + slot, slot)

        @block.vector
        def _(eng):
            steps = [0]

            def done(ins):
                steps[0] += 1
                ins.then_inc(dve, 1)
                eng.wait_ge(dve, steps[0])

            def over(ap, shape):
                return ap.to_broadcast(shape)

            eng.wait_ge(ctx_done, 1)
            eng.wait_ge(gexp, 1)
            for half in range(2):
                last = nc.vector.tensor_scalar(bias_all[:].rearrange("p (n h) -> p n h", h=2)[:, :, half],
                                               sel_ps[:, N * half:N * (half + 1)], biasc[:, half:half + 1], None, ALU.add)
            last.then_inc(bias_ready, 1)
            done(nc.vector.tensor_scalar(g_s[:, 1:2], g_s[:, 0:1], 1.0, None, ALU.add))
            done(nc.vector.reciprocal(g_s[:, 2:3], g_s[:, 1:2]))
            done(nc.vector.tensor_scalar(g_s[:, 3:4], g_s[:, 2:3], -1.0, 1.0, ALU.mult, ALU.add))
            done(nc.vector.tensor_scalar(g_eye[:], eye4, g_s[:, 3:4], None, ALU.mult))

            def softmaxes(c):
                u = slice(CU * c, CU * (c + 1))
                eng.wait_ge(raw_ready, 2 * (c + 1))
                done(nc.vector.tensor_tensor(t_s[:], raw_s[:, u, :], over(bmask.unsqueeze(1), [P, CU, UB]), ALU.mult))
                done(nc.vector.tensor_reduce(ss[:], t_s[:], AX.X, ALU.add))
                nc.vector.tensor_scalar(ms[:], ss[:], 1.0 / L, RMS_EPS, ALU.mult, ALU.add).then_inc(ms_ready, 1)
                eng.wait_ge(rt_ready, c + 1)
                done(nc.vector.reciprocal(inv[:], rt[:]))
                done(nc.vector.tensor_tensor(lg[:], raw_l[:, u, :], over(inv[:].unsqueeze(2), [P, CU, NE]), ALU.mult))
                done(nc.vector.tensor_tensor(lg[:], lg[:], over(base_s[:].unsqueeze(1), [P, CU, NE]), ALU.add))
                groups = CU * NE // NS
                lg4 = lg[:].rearrange("p u (r j) -> p (u r) j", j=NS)
                la4 = la[:].rearrange("p u (r j) -> p (u r) j", j=NS)
                done(nc.vector.tensor_reduce(gmax[:], lg4, AX.X, ALU.max))
                done(nc.vector.tensor_tensor(la4, lg4, over(gmax[:].unsqueeze(2), [P, groups, NS]), ALU.subtract))
                la_h = la[:, :, 0:HH]
                done(nc.vector.tensor_reduce(colmax[:], la_h.rearrange("p u (i j) -> p u j i", j=NS), AX.X, ALU.max))
                done(nc.vector.tensor_tensor(zb[:].rearrange("p i u j -> p u i j"),
                                             la_h.rearrange("p u (i j) -> p u i j", j=NS),
                                             over(colmax[:].unsqueeze(2), [P, CU, NS, NS]), ALU.subtract))
                nc.vector.tensor_scalar(zc[:], zb[:], CLAMP, None, ALU.min).then_inc(args_ready, 1)
                eng.wait_ge(exps_ready, c + 1)
                done(nc.vector.tensor_reduce(s_a[:].rearrange("p i u -> p u i"),
                                             e_h[:].rearrange("p u (i j) -> p u i j", j=NS), AX.X, ALU.add))
                done(nc.vector.reciprocal(r_a[:], s_a[:]))
                done(nc.vector.tensor_reduce(s_p[:], e_p[:].rearrange("p u (r j) -> p (u r) j", j=NS), AX.X, ALU.add))
                done(nc.vector.reciprocal(r_p[:], s_p[:]))
                done(nc.vector.tensor_tensor(soft[:, u, :].rearrange("p u (r j) -> p (u r) j", j=NS),
                                             e_p[:].rearrange("p u (r j) -> p (u r) j", j=NS),
                                             over(r_p[:].unsqueeze(2), [P, 2 * CU, NS]), ALU.mult))
                done(nc.vector.scalar_tensor_tensor(sk[:], p_a[:], BIG, p_b[:], ALU.mult, ALU.max))
                done(nc.vector.tensor_tensor(sk_row, sk_row, over(r_a[:].rearrange("p i u -> p (i u)").unsqueeze(2),
                                                                  [P, NS * CU, NS]), ALU.mult))

            sk_row = sk[:].rearrange("p i u j -> p (i u) j")
            sk_col = sk[:].rearrange("p i u j -> p (u j) i")
            sk_rows = sk[:].rearrange("p i u j -> p i (u j)")

            def row_step(at):
                nc.vector.tensor_reduce(sk_s[:], sk_row, AX.X, ALU.add).then_inc(dve, 1)
                eng.wait_ge(dve, at + 1)
                nc.vector.reciprocal(sk_r[:], sk_s[:]).then_inc(dve, 1)
                eng.wait_ge(dve, at + 2)
                nc.vector.scalar_tensor_tensor(sk_row, over(sk_r[:].unsqueeze(2), [P, NS * CU, NS]), BIG, sk_row,
                                               ALU.mult, ALU.mult).then_inc(dve, 1)
                eng.wait_ge(dve, at + 3)

            def col_step(at):
                nc.vector.tensor_reduce(sk_s[:], sk_col, AX.X, ALU.add).then_inc(dve, 1)
                eng.wait_ge(dve, at + 1)
                nc.vector.reciprocal(sk_r[:], sk_s[:]).then_inc(dve, 1)
                eng.wait_ge(dve, at + 2)
                nc.vector.scalar_tensor_tensor(sk_rows, over(sk_r[:].unsqueeze(1), [P, NS, NS * CU]), BIG, sk_rows,
                                               ALU.mult, ALU.mult).then_inc(dve, 1)
                eng.wait_ge(dve, at + 3)

            def sinkhorn():
                col_step(steps[0])
                at = steps[0] + 3
                with eng.Fori(0, SINK_ITERS - 1) as i:
                    row_step(6 * i + at)
                    col_step(6 * i + at + 3)
                steps[0] = at + 6 * (SINK_ITERS - 1)

            def res_to_pe(c):
                hk4 = hk[:].rearrange("p u (i j) -> p u i j", j=NS)
                done(nc.vector.tensor_scalar(hk4, sk[:].rearrange("p i u j -> p u i j"), 1.0 / BIG, g_s[:, 2:3],
                                             ALU.mult, ALU.mult))
                done(nc.vector.tensor_tensor(hk[:], hk[:], over(g_eye[:].unsqueeze(1), [P, CU, HH]), ALU.add))
                nc.vector.tensor_tensor(mv_h[:], over(hk[:].unsqueeze(2), [P, CU, UB, HH]),
                                        over(bmask.unsqueeze(1).unsqueeze(3), [P, CU, UB, HH]),
                                        ALU.mult).then_inc(mvh_ready, 1)

            jmask = bmask

            def res_from_pe(c):
                eng.wait_ge(xfh_done, c + 1)
                n = CU * UB * NS
                done(nc.vector.tensor_tensor(xf_h[:], xfh_ps[:, :].rearrange("p (n j) -> p n j", j=NS),
                                             over(jmask.unsqueeze(1), [P, n, NS]), ALU.mult))
                nc.vector.tensor_reduce(coef[:, CU * UB * c:CU * UB * (c + 1), :].rearrange("p b i -> p (b i)"),
                                        xf_h[:], AX.X, ALU.add).then_inc(coef_ready, 1)

            softmaxes(0)
            sinkhorn()
            softmaxes_second = softmaxes
            res_to_pe(0)
            softmaxes_second(1)
            nc.vector.tensor_tensor(mv_p[:], over(soft[:, :, 0:NS].unsqueeze(2), [P, NU, UB, NS]),
                                    over(bmask.unsqueeze(1).unsqueeze(3), [P, NU, UB, NS]),
                                    ALU.mult).then_inc(mvp_ready, 1)
            eng.wait_ge(xfp_done, 1)
            done(nc.vector.tensor_tensor(xf_p[:], xfp_ps[:, 0:NBLK * NS].rearrange("p (n j) -> p n j", j=NS),
                                         over(jmask.unsqueeze(1), [P, NBLK, NS]), ALU.mult))
            nc.vector.tensor_reduce(coef_p[:], xf_p[:], AX.X, ALU.add).then_inc(pre_ready, 1)
            res_from_pe(0)
            sinkhorn()
            res_to_pe(1)
            res_from_pe(1)

            def mix_out(u, slot):
                eng.wait_ge(r_loaded[slot], 8 * NS * (u - slot) + 16 * NS)
                for bp in range(2):
                    eng.wait_ge(mix_done, 2 * u + bp + 1)
                    last = nc.vector.tensor_tensor(ost[:, slot, 2 * bp:2 * bp + 2, :],
                                                   mix_ps[slot][bp][:, :].rearrange("p (b c) -> p b c", b=2),
                                                   xres[:, slot, 2 * bp:2 * bp + 2, :], ALU.add)
                    last.then_inc(mix_read[1], 1)
                eng.wait_ge(mix_read[1], 2 * (u - CU) + 2)
                eng.sem_inc(sum_ready[1], 1)

            with eng.Fori(CU // 2, NU // 2) as i:
                for slot in range(2):
                    eng.wait_ge(stored[slot], 16 * NS * i)
                    mix_out(2 * i + slot, slot)


_OUT_SHAPE = (32, 64, 1024)


def kernel(x, cond_128, fside_S_0, L0_cond_weight, L0_cond_c_weight, L0_ffn_W_res, L0_ffn_W_pre, L0_ffn_W_post,
           L0_ffn_H_res_base, L0_ffn_H_pre_base, L0_ffn_H_post_base, L0_ffn_gate, L0_ffn_W_branch):
    import concourse.bacc as _bacc
    from concourse import mybir as _mybir
    from concourse.bass_utils import run_bass_kernel_spmd as _run

    x = np.ascontiguousarray(x)
    cw = np.asarray(L0_cond_weight)
    co_n, gi, taps = cw.shape
    conv_w = np.zeros((3, 32, 2, 3, 32), cw.dtype)
    for half in range(2):
        for g in range(2):
            blk = cw[32 * half + 16 * g:32 * half + 16 * (g + 1)].reshape(16, 16, 3, 3)
            conv_w[:, 16 * g:16 * (g + 1), half, :, 16 * g:16 * (g + 1)] = blk.transpose(3, 1, 2, 0)
    conv_w = conv_w.reshape(96, 2, 3, 32)
    ctx_w = np.ascontiguousarray(np.tile(np.asarray(L0_cond_c_weight).T.reshape(128, 2, 1, 32), (1, 1, 4, 1))
                                 .reshape(128, 2, 128))
    cond_t = np.ascontiguousarray(np.asarray(cond_128).T)
    bias_c = np.ascontiguousarray(np.tile(np.asarray(fside_S_0).reshape(2, 32), (1, 4)).T)
    w_all = np.concatenate([np.asarray(L0_ffn_W_res), np.asarray(L0_ffn_W_pre), np.asarray(L0_ffn_W_post)], axis=0)
    proj_w = np.zeros((128, 2, 4, 32), w_all.dtype)
    proj_w[:, :, :, 0:24] = w_all.reshape(24, 4, 2, 128).transpose(3, 2, 1, 0)
    branch_w = np.ascontiguousarray(np.asarray(L0_ffn_W_branch).reshape(2, 128, 256).transpose(1, 0, 2))
    base = np.concatenate([np.asarray(L0_ffn_H_res_base).reshape(-1), np.asarray(L0_ffn_H_pre_base),
                           np.asarray(L0_ffn_H_post_base)])
    base = np.ascontiguousarray(np.broadcast_to(base[None], (128, 24)))
    gate = np.ascontiguousarray(np.broadcast_to(np.asarray(L0_ffn_gate).reshape(1, 1), (128, 1)))
    consts = np.zeros((128, 2 * 128 + 8 + 24 + 16), np.float32)
    consts[:, 0:128] = np.eye(128)
    consts[:, 128:256] = np.tile(np.eye(32), (4, 4))
    consts[:, 256:260] = np.repeat(np.eye(4), 32, axis=0)
    consts[:, 264:288] = np.tile(np.eye(32)[:, 0:24], (4, 1))
    consts[:, 288:304] = np.eye(4).reshape(1, 16)

    nc = _bacc.Bacc("TRN2", target_bir_lowering=False, num_devices=1)
    f32 = _mybir.dt.float32
    feeds, args = {}, []
    for name, a in (("x", x), ("conv_w", conv_w), ("ctx_w", ctx_w), ("cond_t", cond_t), ("bias_c", bias_c),
                    ("proj_w", proj_w), ("branch_w", branch_w), ("base", base), ("gate", gate), ("consts", consts)):
        feeds[f"in_{name}"] = a
        args.append(nc.dram_tensor(f"in_{name}", a.shape, f32, kind="ExternalInput").ap())
    out = nc.dram_tensor("out_0", _OUT_SHAPE, f32, kind="ExternalOutput").ap()
    adaln_ffn_program(nc, args[0], out, *args[1:])
    r = _run(nc, [feeds], core_ids=[0])
    return r.results[0]["out_0"]
```

```python
import numpy as np


def adaln_ffn_program(nc, x, out, conv_w, ctx_w, cond_t, bias_c, proj_w, branch_w, base, gate, consts):
    import concourse.bass as bass
    from concourse import mybir
    from contextlib import ExitStack

    f32 = mybir.dt.float32
    ALU = mybir.AluOpType
    ACT = mybir.ActivationFunctionType
    AX = mybir.AxisListType
    ds = bass.ds

    N, CH, L = x.shape
    P = 128
    BT = 32
    NS = 4
    C = L // NS
    NBLK = N * CH // BT
    UB = 4
    NU = NBLK // UB
    QU = 4
    NQ = NU // QU
    HU = NU // 2
    TS, TQ = 3, 3
    PAD = 4
    XW = L + 2 * PAD - TS + 1
    NE = NS * NS + 2 * NS
    HH = NS * NS
    SINK_ITERS = 50
    ITER_BODY = 7
    PLAN = [11, 2, 2, 10, 2, 2, 5, 2, 8, 4]
    WARM_START, WARM_END = 4, 5
    TAU_INV = 10.0
    RMS_EPS = 1.1920929e-07
    BIG = float(2.0 ** 120)
    LN_BIG = float(120.0 * np.log(2.0))
    CLAMP = -8.0

    with ExitStack() as ctx:
        def sb(name, shape):
            return ctx.enter_context(nc.sbuf_tensor(name, shape, f32))

        def pb(name):
            return ctx.enter_context(nc.psum_tensor(name, [P, 512], f32))

        def sem(name):
            return ctx.enter_context(nc.semaphore(name))

        cst = sb("cst", [P, 2 * P + 8 + NE + HH])
        ident = cst[:, 0:P]
        tok4 = cst[:, P:2 * P]
        bmask = cst[:, 2 * P:2 * P + 4]
        select = cst[:, 2 * P + 8:2 * P + 8 + NE]
        eye4 = cst[:, 2 * P + 8 + NE:2 * P + 8 + NE + HH]
        convw = sb("convw", [TS * BT, 2, TQ, BT])
        projw = sb("projw", [P, 2, NS, BT])
        branchw = sb("branchw", [P, 2, C])
        ctxw = sb("ctxw", [P, 2, P])
        condt = sb("condt", [P, N])
        biasc = sb("biasc", [P, 2])
        base_s = sb("base_s", [P, NE])
        gate_s = sb("gate_s", [P, 1])
        bias_all = sb("bias_all", [P, NBLK])
        g_s = sb("g_s", [P, 4])
        g_eye = sb("g_eye", [P, HH])
        lnbig = sb("lnbig", [P, 1])

        xin_all = sb("xin", [P, QU * UB * XW])
        xin = xin_all[0:TS * BT, :].rearrange("p (k b w) -> p k b w", k=QU, b=UB)
        part = xin_all[:, 0:HU * UB * C].rearrange("p (u b c) -> p u b c", u=HU, b=UB)
        h_now = sb("h_now", [P, 2, UB, C])
        h_all = sb("h_all", [P, NBLK, C])
        ht_y = sb("ht_y", [P, 2 * QU * 512])
        ht = ht_y[:, :].rearrange("p (a k n) -> p a k n", a=2, k=QU)
        y_all = ht_y[:, :].rearrange("p (u c) -> p u c", u=NU)
        sq_junk = sb("sq_junk", [P, 2, C])
        zeros = sb("zeros", [P, 512])
        ssq = sb("ssq", [P, NBLK])
        lp_s = sb("lp_s", [P, 512])
        raw_l = sb("raw_l", [P, NU, NE])
        raw_s = sb("raw_s", [P, NU, UB])

        t_s = sb("t_s", [P, QU, UB])
        ss = sb("ss", [P, QU])
        ms = sb("ms", [P, QU])
        rt = sb("rt", [P, QU])
        inv = sb("inv", [P, QU])
        lg = sb("lg", [P, QU, NE])
        la = sb("la", [P, QU, NE])
        gmax = sb("gmax", [P, QU * NE // NS])
        colmax = sb("colmax", [P, QU, NS])
        zb = sb("zb", [P, NS, QU, NS])
        zc = sb("zc", [P, NS, QU, NS])
        e_h = sb("e_h", [P, QU, HH])
        e_p = sb("e_p", [P, QU, 2 * NS])
        p_a = sb("p_a", [P, NS, QU, NS])
        p_b = sb("p_b", [P, NS, QU, NS])
        s_a = sb("s_a", [P, NS, QU])
        r_a = sb("r_a", [P, NS, QU])
        s_p = sb("s_p", [P, 2 * QU])
        r_p = sb("r_p", [P, 2 * QU])
        soft = sb("soft", [P, NU, 2 * NS])
        sk = [sb(f"sk{q}", [P, NS, QU, NS]) for q in range(NQ)]
        sk_s = [sb(f"sk_s{q}", [P, NS * QU]) for q in range(NQ)]
        sk_r = [sb(f"sk_r{q}", [P, NS * QU]) for q in range(NQ)]
        hk = sb("hk", [P, QU, HH])
        mv_h = sb("mv_h", [P, 2, QU, UB, HH])
        mv_p = sb("mv_p", [P, NU, UB, NS])
        xf_h = sb("xf_h", [P, QU * UB * NS, NS])
        xf_p = sb("xf_p", [P, NBLK // 2, NS])
        coef = sb("coef", [P, NBLK, NS])
        coef_p = sb("coef_p", [P, NBLK])

        pre_m = sb("pre_m", [P, 2, UB, BT])
        res_m = sb("res_m", [P, 2, UB, NS, BT])
        post_m = sb("post_m", [P, 2, UB, NS, BT])
        xp_s = sb("xp_s", [P, 2, C])
        xpt_s = sb("xpt_s", [P, 2, C])
        xres = sb("xres", [P, 2, UB, C])
        ost = h_now

        banks = [pb(f"bank{i}") for i in range(8)]
        conv_ps = [banks[0], banks[1]]
        ht_ps = [banks[2], banks[3]]
        lp_ps = banks[4]
        sel_ps = banks[5]
        xp_ps, xpt_ps, y_ps = banks[2], banks[3], banks[4]
        mix_ps = [[banks[0], banks[1]], [banks[6], banks[7]]]
        xfp_ps, xfh_ps = banks[2], [banks[5], banks[5], banks[5], banks[4]]

        convw_loaded = sem("convw_loaded")
        zeros_ready = sem("zeros_ready")
        sink_near = sem("sink_near")
        ctx_loaded = sem("ctx_loaded")
        w_loaded = sem("w_loaded")
        x_margin = sem("x_margin")
        x_first = sem("x_first")
        x_loaded = [sem(f"x_loaded{k}") for k in range(QU)]
        conv_done = sem("conv_done")
        h_ready = sem("h_ready")
        conv_read = sem("conv_read")
        h_kept = sem("h_kept")
        t_done = sem("t_done")
        ht_ready = sem("ht_ready")
        logit_done = sem("logit_done")
        lp_ready = sem("lp_ready")
        sel_done = sem("sel_done")
        raw_ready = sem("raw_ready")
        ctx_done = sem("ctx_done")
        bias_ready = sem("bias_ready")
        gexp = sem("gexp")
        dve = sem("dve")
        sink = sem("sink")
        ms_ready = sem("ms_ready")
        rt_ready = sem("rt_ready")
        args_ready = sem("args_ready")
        exps_ready = sem("exps_ready")
        mvp_ready = sem("mvp_ready")
        mvh_ready = sem("mvh_ready")
        xfp_done = sem("xfp_done")
        xfh_done = sem("xfh_done")
        pre_ready = sem("pre_ready")
        coef_ready = sem("coef_ready")
        pre_built = sem("pre_built")
        xp_done = sem("xp_done")
        xp_ready = sem("xp_ready")
        xpt_done = sem("xpt_done")
        xpt_ready = sem("xpt_ready")
        y_done = sem("y_done")
        y_ready = sem("y_ready")
        post_built = sem("post_built")
        res_built = sem("res_built")
        mix_done = sem("mix_done")
        mix_read = sem("mix_read")
        x_added = sem("x_added")
        end_done = sem("end_done")
        end_read = sem("end_read")
        r_loaded = [sem(f"r_loaded{k}") for k in range(2)]
        stored = [sem(f"stored{k}") for k in range(2)]

        W_LOADS = 4

        x_cv = x.rearrange("n (h c) l -> c (n h) l", h=2)
        x_tok = x.rearrange("n (h c) (j l) -> j c (n h) l", h=2, j=NS)
        o_tok = out.rearrange("n (h c) (j l) -> j c (n h) l", h=2, j=NS)

        block = ctx.enter_context(nc.Block())

        @block.sync
        def _(sp):
            def load_unit(u, k):
                for s in range(TS):
                    sp.dma_start(xin[BT * s:BT * (s + 1), k, :, PAD - s:PAD - s + L],
                                 x_cv[:, ds(UB * u, UB), :]).then_inc(x_loaded[k], 16)

            def load_res(u, slot):
                for j in range(NS):
                    sp.dma_start(xres[BT * j:BT * (j + 1), slot, :, :],
                                 x_tok[j, :, ds(UB * u, UB), :]).then_inc(r_loaded[slot], 16)

            def store(u, tile, slot):
                for j in range(NS):
                    sp.dma_start(o_tok[j, :, ds(UB * u, UB), :],
                                 tile[BT * j:BT * (j + 1), :, :]).then_inc(stored[slot], 16)

            sp.wait_ge(x_margin, 1)
            for half, signal in ((0, x_first), (1, x_loaded[0])):
                for s in range(TS):
                    sp.dma_start(xin[BT * s:BT * (s + 1), 0, half::2, PAD - s:PAD - s + L],
                                 x_cv[:, half:UB:2, :]).then_inc(signal, 16)
            for k in range(1, QU):
                load_unit(k, k)
            with sp.Fori(1, NQ) as i:
                for k in range(QU):
                    sp.wait_ge(conv_done, 2 * QU * i + 2 * (k + 1 - QU))
                    load_unit(QU * i + k, k)
            for slot in range(2):
                load_res(slot, slot)
            with sp.Fori(0, HU // 2) as i:
                for slot in range(2):
                    sp.wait_ge(x_added, 2 * i + slot + 1)
                    store(2 * i + slot, ost[:, slot], slot)
                    load_res(2 * i + slot + 2, slot)
            with sp.Fori(HU // 2, NU // 2 - 1) as i:
                for slot in range(2):
                    sp.wait_ge(x_added, 2 * i + slot + 1)
                    load_res(2 * i + slot + 2, slot)
            with sp.Fori(0, HU // 2) as i:
                for slot in range(2):
                    sp.wait_ge(end_read, 4 * i + 2 * slot + 2)
                    store(HU + 2 * i + slot, part[:, ds(2 * i + slot, 1)].rearrange("p u b c -> p (u b) c"), slot)
            for slot in range(2):
                sp.wait_ge(stored[slot], 16 * NS * NU // 2)

        @block.tensor
        def _(pe):
            def conv(u, k, i, half, first=False):
                if first and k == 0 and half == 0:
                    pe.wait_ge(x_first, 16 * TS)
                elif half == 0 or (first and k == 0):
                    pe.wait_ge(x_loaded[k], 16 * TS * (i + 1))
                if not first:
                    pe.wait_ge(conv_read, 2 * u + half - 1)
                for q in range(TQ):
                    for j in range(NS):
                        last = nc.tensor.matmul(conv_ps[half][BT * j:BT * (j + 1), :].rearrange("p (b c) -> p b c", b=2),
                                                convw[:, half, q, :],
                                                xin[:, k, half::2, C * j + TS * q:C * j + TS * q + C],
                                                start=(q == 0), stop=(q == TQ - 1))
                last.then_inc(conv_done, 1)

            def transpose_h(u, slot, first=False):
                pe.wait_ge(h_ready, 2 * u + 2)
                for a in range(2):
                    if not first:
                        pe.wait_ge(ht_ready, 2 * u + a - 1)
                    for b in range(UB):
                        last = nc.tensor.transpose(ht_ps[a][:, P * b:P * (b + 1)],
                                                   h_now[:, slot, b, P * a:P * (a + 1)], ident)
                    last.then_inc(t_done, 1)

            def logits(i):
                pe.wait_ge(ht_ready, 2 * QU * (i + 1))
                for a in range(2):
                    hv = ht[:, a].rearrange("p k (b j t) -> p (k b) j t", b=UB, j=NS)
                    for j in range(NS):
                        last = nc.tensor.matmul(lp_ps[BT * j:BT * (j + 1), :], projw[:, a, j, :], hv[:, :, j, :],
                                                start=(a == 0), stop=(a == 1))
                last.then_inc(logit_done, 1)

            def to_tokens(i):
                pe.wait_ge(lp_ready, i + 1)
                for k in range(QU):
                    nc.tensor.matmul(sel_ps[:, NE * k:NE * (k + 1)], lp_s[:, P * k:P * (k + 1)], select,
                                     start=True, stop=True)
                nc.tensor.matmul(sel_ps[:, NE * QU:NE * QU + UB * QU], tok4, ssq[:, ds(UB * QU * i, UB * QU)],
                                 start=True, stop=True).then_inc(sel_done, 1)

            def keep_warm(n):
                for m in range(n):
                    nc.tensor.matmul(banks[3][:, :], zeros[:, 0:P], zeros[:, :], start=True, stop=True)

            def context():
                pe.wait_ge(ctx_loaded, 16 * 4)
                for half in range(2):
                    last = nc.tensor.matmul(sel_ps[:, N * half:N * (half + 1)], ctxw[:, half, :], condt[:],
                                            start=True, stop=True)
                last.then_inc(ctx_done, 1)

            def quad(i, first):
                u = QU * i
                conv(u, 0, i, 0, first=first)
                if first:
                    context()
                else:
                    transpose_h(u - 1, 1)
                conv(u, 0, i, 1, first=first)
                if not first:
                    logits(i - 1)
                conv(u + 1, 1, i, 0)
                if not first:
                    to_tokens(i - 1)
                conv(u + 1, 1, i, 1)
                if first:
                    pe.wait_ge(w_loaded, 16 * W_LOADS)
                transpose_h(u, 0, first=first)
                for k in (2, 3):
                    conv(u + k, k, i, 0)
                    conv(u + k, k, i, 1)
                    transpose_h(u + k - 1, (k - 1) % 2)

            def x_pre(u, slot, first=False):
                pe.wait_ge(pre_built, u + 1)
                if not first:
                    pe.wait_ge(xp_ready, u)
                for b in range(UB):
                    last = nc.tensor.matmul(xp_ps[BT * b:BT * (b + 1), 0:C], pre_m[:, slot, b, :],
                                            h_all[:, UB * u + b, :], start=True, stop=True)
                last.then_inc(xp_done, 1)

            def x_pre_t(u, slot, first=False):
                pe.wait_ge(xp_ready, u + 1)
                if not first:
                    pe.wait_ge(xpt_ready, u)
                for a in range(2):
                    last = nc.tensor.transpose(xpt_ps[:, P * a:P * (a + 1)],
                                               xp_s[:, slot, P * a:P * (a + 1)], ident)
                last.then_inc(xpt_done, 1)

            def branch(u, slot, first=False):
                pe.wait_ge(xpt_ready, u + 1)
                if not first:
                    pe.wait_ge(y_ready, u)
                for a in range(2):
                    last = nc.tensor.matmul(y_ps[:, 0:C], xpt_s[:, slot, P * a:P * (a + 1)],
                                            branchw[:, a, :], start=(a == 0), stop=(a == 1))
                last.then_inc(y_done, 1)

            def branch_half(c):
                for t in range(HU * c, HU * (c + 1) + 2):
                    if t < HU * (c + 1):
                        x_pre(t, t % 2, t == 0)
                    if HU * c <= t - 1 < HU * (c + 1):
                        x_pre_t(t - 1, (t - 1) % 2, t - 1 == 0)
                    if t - 2 >= HU * c:
                        branch(t - 2, t % 2, t - 2 == 0)

            def mix(u, slot, res, first=False):
                pe.wait_ge(post_built, u + 1)
                if res:
                    pe.wait_ge(res_built, u + 1)
                pe.wait_ge(y_ready, u + 1)
                for bp in range(2):
                    if not first:
                        pe.wait_ge(mix_read, 2 * u + bp - 3)
                    for b in (2 * bp, 2 * bp + 1):
                        o = mix_ps[slot][bp][:, C * (b % 2):C * (b % 2 + 1)]
                        if res:
                            nc.tensor.matmul(o, res_m[:, slot, b], h_all[:, ds(UB * u + b, 1), :],
                                             start=True, stop=False)
                        last = nc.tensor.matmul(o, post_m[:, slot, b], y_all[:, ds(u, 1), :],
                                                start=not res, stop=True)
                    last.then_inc(mix_done, 1)

            def end(u, slot, first=False):
                pe.wait_ge(res_built, u + HU + 1)
                for bp in range(2):
                    if not first:
                        pe.wait_ge(end_read, 2 * u + bp - 3)
                    for b in (2 * bp, 2 * bp + 1):
                        last = nc.tensor.matmul(mix_ps[slot][bp][:, C * (b % 2):C * (b % 2 + 1)], res_m[:, slot, b],
                                                h_all[:, ds(UB * (u + HU) + b, 1), :], start=True, stop=True)
                    last.then_inc(end_done, 1)

            def spread_pre(c):
                pe.wait_ge(mvp_ready, 2 * (c + 1))
                nc.tensor.matmul(xfp_ps[:, 0:HU * UB * NS], tok4,
                                 mv_p[:, HU * c:HU * (c + 1)].rearrange("p u b e -> p (u b e)"),
                                 start=True, stop=True).then_inc(xfp_done, 1)

            def spread_res(q):
                pe.wait_ge(mvh_ready, q + 1)
                nc.tensor.matmul(xfh_ps[q][:, 0:QU * UB * HH], tok4,
                                 mv_h[:, q % 2].rearrange("p u b e -> p (u b e)"),
                                 start=True, stop=True).then_inc(xfh_done, 1)

            pe.wait_ge(zeros_ready, 1)
            keep_warm(WARM_START)
            pe.wait_ge(convw_loaded, 16)
            quad(0, True)
            with pe.Fori(1, NQ) as i:
                quad(i, False)
            transpose_h(NU - 1, 1)
            logits(NQ - 1)
            to_tokens(NQ - 1)
            spread_pre(0)
            branch_half(0)
            spread_res(0)
            for slot in range(2):
                mix(slot, slot, True, first=True)
            with pe.Fori(1, QU // 2) as i:
                for slot in range(2):
                    mix(2 * i + slot, slot, True)
            spread_pre(1)
            branch_half(1)
            spread_res(1)
            with pe.Fori(QU // 2, HU // 2) as i:
                for slot in range(2):
                    mix(2 * i + slot, slot, True)
            with pe.Fori(HU // 2, NU // 2) as i:
                for slot in range(2):
                    mix(2 * i + slot, slot, False)
            pe.wait_ge(mix_read, 2 * NU)
            pe.wait_ge(sink_near, 1)
            keep_warm(WARM_END)
            spread_res(2)
            spread_res(3)
            for slot in range(2):
                end(slot, slot, first=True)
            with pe.Fori(1, HU // 2) as i:
                for slot in range(2):
                    end(2 * i + slot, slot)

        @block.scalar
        def _(act):
            def conv_out(u, slot, half, first=False):
                if half == 0 and not first:
                    act.wait_ge(t_done, 2 * u - 2)
                    act.wait_ge(h_kept, u - 1)
                act.wait_ge(conv_done, 2 * u + half + 1)
                for n in range(2):
                    b = 2 * n + half
                    last = nc.scalar.activation(h_now[:, slot, b, :], conv_ps[half][:, C * n:C * (n + 1)], ACT.Identity,
                                                bias=bias_all[:, ds(UB * u + b, 1)])
                last.then_inc(h_ready, 1)
                if not first or half or slot:
                    act.wait_ge(conv_read, 2 * u + half)
                for n in range(2):
                    b = UB * u + 2 * n + half
                    last = nc.scalar.activation(sq_junk[:, n, :], conv_ps[half][:, C * n:C * (n + 1)], ACT.Square,
                                                bias=bias_all[:, ds(b, 1)], accum_out=ssq[:, ds(b, 1)])
                last.then_inc(conv_read, 1)

            def ht_out(u, k, i, first=False):
                for a in range(2):
                    act.wait_ge(t_done, 2 * u + a + 1)
                    if not first:
                        act.wait_ge(logit_done, i)
                    nc.scalar.copy(ht[:, a, k, :], ht_ps[a][:, :]).then_inc(ht_ready, 1)

            def logits_out(i, first=False):
                act.wait_ge(logit_done, i + 1)
                if not first:
                    act.wait_ge(sel_done, i)
                nc.scalar.copy(lp_s[:], lp_ps[:, :]).then_inc(lp_ready, 1)

            def tokens_out(i):
                act.wait_ge(sel_done, i + 1)
                nc.scalar.copy(raw_l[:, ds(QU * i, QU), :],
                               sel_ps[:, 0:NE * QU].rearrange("p (k e) -> p k e", e=NE))
                nc.scalar.copy(raw_s[:, ds(QU * i, QU), :],
                               sel_ps[:, NE * QU:(NE + UB) * QU].rearrange("p (k e) -> p k e", e=UB)).then_inc(raw_ready, 1)

            def root(c):
                act.wait_ge(ms_ready, c + 1)
                nc.scalar.activation(rt[:], ms[:], ACT.Sqrt).then_inc(rt_ready, 1)

            def exponentials(c):
                act.wait_ge(args_ready, c + 1)
                nc.scalar.activation(e_h[:], la[:, :, 0:HH], ACT.Exp, scale=TAU_INV)
                nc.scalar.activation(e_p[:], la[:, :, HH:NE], ACT.Exp)
                nc.scalar.activation(p_a[:], zb[:], ACT.Exp, scale=TAU_INV)
                nc.scalar.activation(p_b[:], zc[:], ACT.Exp, scale=TAU_INV, bias=lnbig[:, 0:1]).then_inc(exps_ready, 1)

            def quad(i, last_quad):
                u = QU * i
                first = last_quad is None
                conv_out(u, 0, 0, first)
                if last_quad:
                    ht_out(u - 1, 3, i - 1, *last_quad)
                conv_out(u, 0, 1, first)
                if last_quad:
                    logits_out(i - 1, *last_quad)
                conv_out(u + 1, 1, 0, first)
                if last_quad:
                    tokens_out(i - 1)
                conv_out(u + 1, 1, 1, first)
                if last_quad:
                    root(i - 1)
                ht_out(u, 0, i, first)
                conv_out(u + 2, 0, 0)
                if last_quad:
                    exponentials(i - 1)
                conv_out(u + 2, 0, 1)
                ht_out(u + 1, 1, i, first)
                conv_out(u + 3, 1, 0)
                conv_out(u + 3, 1, 1)
                ht_out(u + 2, 2, i, first)

            def x_pre_out(u, slot, first=False):
                act.wait_ge(xp_done, u + 1)
                if not first:
                    act.wait_ge(xpt_done, u - 1)
                nc.scalar.copy(xp_s[:, slot, :], xp_ps[:, 0:C]).then_inc(xp_ready, 1)

            def x_pre_t_out(u, slot, first=False):
                act.wait_ge(xpt_done, u + 1)
                if not first:
                    act.wait_ge(y_done, u - 1)
                nc.scalar.copy(xpt_s[:, slot, :], xpt_ps[:, 0:C]).then_inc(xpt_ready, 1)

            def branch_out(u, slot):
                act.wait_ge(y_done, u + 1)
                nc.scalar.copy(y_all[:, ds(u, 1), :], y_ps[:, 0:C]).then_inc(y_ready, 1)

            def branch_half(c):
                u = HU * c
                x_pre_out(u, 0, c == 0)
                x_pre_out(u + 1, 1, c == 0)
                x_pre_t_out(u, 0, c == 0)
                x_pre_out(u + 2, 0)
                x_pre_t_out(u + 1, 1, c == 0)
                branch_out(u, 0)
                with act.Fori(u // 2 + 1, (u + HU) // 2 - 1) as i:
                    for slot in range(2):
                        x_pre_out(2 * i + slot + 1, 1 - slot)
                        x_pre_t_out(2 * i + slot, slot)
                        branch_out(2 * i + slot - 1, 1 - slot)
                x_pre_out(u + HU - 1, 1)
                x_pre_t_out(u + HU - 2, 0)
                branch_out(u + HU - 3, 1)
                x_pre_t_out(u + HU - 1, 1)
                branch_out(u + HU - 2, 0)
                branch_out(u + HU - 1, 1)

            def mix_out(u, slot, tile):
                for bp in range(2):
                    act.wait_ge(mix_done, 2 * u + bp + 1)
                    nc.scalar.copy(tile(bp), mix_ps[slot][bp][:, :].rearrange("p (b c) -> p b c", b=2)
                                   ).then_inc(mix_read, 1)

            def to_ost(slot):
                return lambda bp: ost[:, slot, 2 * bp:2 * bp + 2, :]

            for dst, src in ((convw, conv_w),):
                act.dma_start(dst[:], src).then_inc(convw_loaded, 16)
            for dst, src in ((ctxw, ctx_w), (condt, cond_t), (biasc, bias_c), (gate_s, gate)):
                act.dma_start(dst[:], src).then_inc(ctx_loaded, 16)
            for dst, src in ((cst, consts), (projw, proj_w), (base_s, base), (branchw, branch_w)):
                act.dma_start(dst[:], src).then_inc(w_loaded, 16)
            act.wait_ge(ctx_loaded, 16 * 4)
            nc.scalar.activation(g_s[:, 0:1], gate_s[:], ACT.Exp, scale=-1.0).then_inc(gexp, 1)
            act.wait_ge(bias_ready, 1)
            quad(0, None)
            quad(1, (True,))
            with act.Fori(2, NQ) as i:
                quad(i, (False,))
            ht_out(NU - 1, 3, NQ - 1)
            logits_out(NQ - 1)
            tokens_out(NQ - 1)
            root(NQ - 1)
            exponentials(NQ - 1)
            branch_half(0)
            act.wait_ge(h_kept, NU)
            for slot in range(2):
                mix_out(slot, slot, to_ost(slot))
            with act.Fori(1, QU // 2) as i:
                for slot in range(2):
                    act.wait_ge(stored[slot], 16 * NS * i)
                    mix_out(2 * i + slot, slot, to_ost(slot))
            branch_half(1)
            with act.Fori(QU // 2, HU // 2) as i:
                for slot in range(2):
                    act.wait_ge(stored[slot], 16 * NS * i)
                    mix_out(2 * i + slot, slot, to_ost(slot))
            with act.Fori(HU // 2, NU // 2) as i:
                for slot in range(2):
                    pu = part[:, ds(2 * i + slot - HU, 1)].rearrange("p u b c -> p (u b) c")
                    mix_out(2 * i + slot, slot, lambda bp: pu[:, 2 * bp:2 * bp + 2, :])

        @block.gpsimd
        def _(pool):
            nc.gpsimd.memset(xin[:, :, :, 0:PAD], 0.0)
            nc.gpsimd.memset(xin[:, :, :, XW - PAD:XW], 0.0).then_inc(x_margin, 1)
            nc.gpsimd.memset(lnbig[:], LN_BIG).then_inc(x_margin, 1)

            with pool.Fori(0, NU // 2) as i:
                for slot in range(2):
                    pool.wait_ge(h_ready, 4 * i + 2 * slot + 2)
                    nc.gpsimd.tensor_copy(h_all[:, ds(UB * (2 * i + slot), UB), :], h_now[:, slot]).then_inc(h_kept, 1)

            lane = tok4[:, 0:BT]

            def build_pre(u, slot, first=False):
                if not first:
                    pool.wait_ge(xp_done, u - 1)
                nc.gpsimd.tensor_tensor(pre_m[:, slot], lane.unsqueeze(1).to_broadcast([P, UB, BT]),
                                        coef_p[:, ds(UB * u, UB)].unsqueeze(2).to_broadcast([P, UB, BT]),
                                        ALU.mult).then_inc(pre_built, 1)

            def build_post(u, slot, first=False):
                if not first:
                    pool.wait_ge(mix_done, 2 * u - 2)
                nc.gpsimd.tensor_tensor(
                    post_m[:, slot],
                    ident.rearrange("p (b t) -> p b t", b=UB).unsqueeze(2).to_broadcast([P, UB, NS, BT]),
                    soft[:, ds(u, 1), NS:2 * NS].rearrange("p u i -> p (u i)").unsqueeze(1).unsqueeze(3)
                    .to_broadcast([P, UB, NS, BT]),
                    ALU.mult).then_inc(post_built, 1)

            def build_res(u, slot, used=None):
                if used is not None:
                    pool.wait_ge(*used)
                nc.gpsimd.tensor_tensor(
                    res_m[:, slot].rearrange("p b i t -> p (b i) t"),
                    lane.unsqueeze(1).to_broadcast([P, UB * NS, BT]),
                    coef[:, ds(UB * u, UB), :].rearrange("p b i -> p (b i)").unsqueeze(2).to_broadcast([P, UB * NS, BT]),
                    ALU.mult).then_inc(res_built, 1)

            def build_mix(u, slot, first=False):
                build_post(u, slot, first)
                build_res(u, slot)

            def add_x(u, slot, tile):
                pool.wait_ge(mix_read, 2 * u + 2)
                pool.wait_ge(r_loaded[slot], 8 * NS * (u - slot) + 16 * NS)
                nc.gpsimd.tensor_tensor(tile, tile, xres[:, slot], ALU.add).then_inc(x_added, 1)

            def of_part(u):
                return part[:, ds(u - HU, 1)].rearrange("p u b c -> p (u b) c")

            pool.wait_ge(pre_ready, 1)
            for slot in range(2):
                build_pre(slot, slot, True)
            with pool.Fori(1, HU // 2) as i:
                for slot in range(2):
                    build_pre(2 * i + slot, slot)
            pool.wait_ge(coef_ready, 1)
            for slot in range(2):
                build_mix(slot, slot, True)
            for u in range(QU - 2):
                add_x(u, u % 2, ost[:, u % 2])
                build_mix(u + 2, u % 2)
            for u in range(QU - 2, QU):
                add_x(u, u % 2, ost[:, u % 2])
            pool.wait_ge(pre_ready, 2)
            with pool.Fori(HU // 2, NU // 2) as i:
                for slot in range(2):
                    build_pre(2 * i + slot, slot)
            pool.wait_ge(coef_ready, 2)
            for u in range(QU, QU + 2):
                build_mix(u, u % 2)
            for u in range(QU, HU - 2):
                add_x(u, u % 2, ost[:, u % 2])
                build_mix(u + 2, u % 2)
            for slot in range(2):
                add_x(HU - 2 + slot, slot, ost[:, slot])
                build_post(HU + slot, slot)
            with pool.Fori(HU // 2, NU // 2 - 1) as i:
                for slot in range(2):
                    u = 2 * i + slot
                    add_x(u, slot, of_part(u))
                    build_post(u + 2, slot)
            for slot in range(2):
                add_x(NU - 2 + slot, slot, of_part(NU - 2 + slot))
            pool.wait_ge(coef_ready, NQ)
            for slot in range(2):
                build_res(HU + slot, slot)
            with pool.Fori(HU // 2 + 1, NU // 2) as i:
                for slot in range(2):
                    build_res(2 * i + slot, slot, (end_done, 4 * i + 2 * slot - 2 * HU - 2))

        @block.vector
        def _(eng):
            steps = [0]

            def done(ins):
                steps[0] += 1
                ins.then_inc(dve, 1)
                eng.wait_ge(dve, steps[0])

            def over(ap, shape):
                return ap.to_broadcast(shape)

            nc.vector.memset(zeros[:], 0.0).then_inc(zeros_ready, 1)
            eng.wait_ge(ctx_done, 1)
            eng.wait_ge(gexp, 1)
            eng.wait_ge(w_loaded, 16 * W_LOADS)
            for half in range(2):
                last = nc.vector.tensor_scalar(bias_all[:].rearrange("p (n h) -> p n h", h=2)[:, :, half],
                                               sel_ps[:, N * half:N * (half + 1)], biasc[:, half:half + 1], None, ALU.add)
            last.then_inc(bias_ready, 1)
            done(nc.vector.tensor_scalar(g_s[:, 1:2], g_s[:, 0:1], 1.0, None, ALU.add))
            done(nc.vector.reciprocal(g_s[:, 2:3], g_s[:, 1:2]))
            done(nc.vector.tensor_scalar(g_s[:, 3:4], g_s[:, 2:3], -1.0, 1.0, ALU.mult, ALU.add))
            done(nc.vector.tensor_scalar(g_eye[:], eye4, g_s[:, 3:4], None, ALU.mult))

            def squares(q):
                eng.wait_ge(raw_ready, q + 1)
                done(nc.vector.tensor_tensor(t_s[:], raw_s[:, QU * q:QU * (q + 1), :],
                                             over(bmask.unsqueeze(1), [P, QU, UB]), ALU.mult))
                done(nc.vector.tensor_reduce(ss[:], t_s[:], AX.X, ALU.add))
                nc.vector.tensor_scalar(ms[:], ss[:], 1.0 / L, RMS_EPS, ALU.mult, ALU.add).then_inc(ms_ready, 1)

            def arguments(q):
                eng.wait_ge(rt_ready, q + 1)
                done(nc.vector.reciprocal(inv[:], rt[:]))
                done(nc.vector.tensor_tensor(lg[:], raw_l[:, QU * q:QU * (q + 1), :],
                                             over(inv[:].unsqueeze(2), [P, QU, NE]), ALU.mult))
                done(nc.vector.tensor_tensor(lg[:], lg[:], over(base_s[:].unsqueeze(1), [P, QU, NE]), ALU.add))
                groups = QU * NE // NS
                lg4 = lg[:].rearrange("p u (r j) -> p (u r) j", j=NS)
                la4 = la[:].rearrange("p u (r j) -> p (u r) j", j=NS)
                done(nc.vector.tensor_reduce(gmax[:], lg4, AX.X, ALU.max))
                done(nc.vector.tensor_tensor(la4, lg4, over(gmax[:].unsqueeze(2), [P, groups, NS]), ALU.subtract))
                la_h = la[:, :, 0:HH]
                done(nc.vector.tensor_reduce(colmax[:], la_h.rearrange("p u (i j) -> p u j i", j=NS), AX.X, ALU.max))
                done(nc.vector.tensor_tensor(zb[:].rearrange("p i u j -> p u i j"),
                                             la_h.rearrange("p u (i j) -> p u i j", j=NS),
                                             over(colmax[:].unsqueeze(2), [P, QU, NS, NS]), ALU.subtract))
                nc.vector.tensor_scalar(zc[:], zb[:], CLAMP, None, ALU.min).then_inc(args_ready, 1)

            def start(q):
                eng.wait_ge(exps_ready, q + 1)
                done(nc.vector.tensor_reduce(s_a[:].rearrange("p i u -> p u i"),
                                             e_h[:].rearrange("p u (i j) -> p u i j", j=NS), AX.X, ALU.add))
                done(nc.vector.reciprocal(r_a[:], s_a[:]))
                done(nc.vector.tensor_reduce(s_p[:], e_p[:].rearrange("p u (r j) -> p (u r) j", j=NS), AX.X, ALU.add))
                done(nc.vector.reciprocal(r_p[:], s_p[:]))
                sq = soft[:, QU * q:QU * (q + 1), :]
                done(nc.vector.tensor_tensor(sq.rearrange("p u (r j) -> p (u r) j", j=NS),
                                             e_p[:].rearrange("p u (r j) -> p (u r) j", j=NS),
                                             over(r_p[:].unsqueeze(2), [P, 2 * QU, NS]), ALU.mult))
                nc.vector.tensor_tensor(mv_p[:, QU * q:QU * (q + 1)], over(sq[:, :, 0:NS].unsqueeze(2), [P, QU, UB, NS]),
                                        over(bmask.unsqueeze(1).unsqueeze(3), [P, QU, UB, NS]),
                                        ALU.mult).then_inc(mvp_ready, 1)
                done(nc.vector.scalar_tensor_tensor(sk[q][:], p_a[:], BIG, p_b[:], ALU.mult, ALU.max))
                done(nc.vector.tensor_tensor(sk[q][:], sk[q][:], over(r_a[:].unsqueeze(3), [P, NS, QU, NS]), ALU.mult))
                normalise(0, False, (q,))
                settle(3, (q,))

            def normalise(at, rows, quads):
                for k in range(3):
                    for n, q in enumerate(quads):
                        if at + k:
                            eng.wait_ge(sink, len(quads) * (at + k - 1) + n + 1)
                        m = sk[q][:]
                        if k == 0:
                            ins = nc.vector.tensor_reduce(sk_s[q][:], m.rearrange("p i u j -> p (i u) j") if rows else
                                                          m.rearrange("p i u j -> p (u j) i"), AX.X, ALU.add)
                        elif k == 1:
                            ins = nc.vector.reciprocal(sk_r[q][:], sk_s[q][:])
                        elif rows:
                            mr = m.rearrange("p i u j -> p (i u) j")
                            ins = nc.vector.scalar_tensor_tensor(mr, over(sk_r[q][:].unsqueeze(2), [P, NS * QU, NS]),
                                                                 BIG, mr, ALU.mult, ALU.mult)
                        else:
                            mc = m.rearrange("p i u j -> p i (u j)")
                            ins = nc.vector.scalar_tensor_tensor(mc, over(sk_r[q][:].unsqueeze(1), [P, NS, NS * QU]),
                                                                 BIG, mc, ALU.mult, ALU.mult)
                        ins.then_inc(sink, 1)

            def settle(n, quads):
                eng.wait_ge(sink, len(quads) * n)
                eng.sem_clear(sink)

            left = [SINK_ITERS - 1] * NQ

            def iterate(quads, n):
                def body(size):
                    for m in range(size):
                        normalise(6 * m, True, quads)
                        normalise(6 * m + 3, False, quads)
                    settle(6 * size, quads)

                for q in quads:
                    left[q] -= n
                if n >= 2 * ITER_BODY:
                    with eng.Fori(0, n // ITER_BODY) as i:
                        body(ITER_BODY)
                    n = n % ITER_BODY
                if n:
                    body(n)

            def res_to_pe(q):
                assert left[q] == 0
                done(nc.vector.tensor_scalar(hk[:].rearrange("p u (i j) -> p u i j", j=NS),
                                             sk[q][:].rearrange("p i u j -> p u i j"), 1.0 / BIG, g_s[:, 2:3],
                                             ALU.mult, ALU.mult))
                done(nc.vector.tensor_tensor(hk[:], hk[:], over(g_eye[:].unsqueeze(1), [P, QU, HH]), ALU.add))
                done(nc.vector.tensor_tensor(mv_h[:, q % 2], over(hk[:].unsqueeze(2), [P, QU, UB, HH]),
                                             over(bmask.unsqueeze(1).unsqueeze(3), [P, QU, UB, HH]), ALU.mult))
                eng.sem_inc(mvh_ready, 1)

            jmask = bmask

            def res_from_pe(q):
                eng.wait_ge(xfh_done, q + 1)
                if q:
                    eng.wait_ge(coef_ready, q)
                n = QU * UB * NS
                done(nc.vector.tensor_tensor(xf_h[:], xfh_ps[q][:, 0:NS * n]
                                             .rearrange("p (n j) -> p n j", j=NS),
                                             over(jmask.unsqueeze(1), [P, n, NS]), ALU.mult))
                nc.vector.tensor_reduce(coef[:, QU * UB * q:QU * UB * (q + 1), :].rearrange("p b i -> p (b i)"),
                                        xf_h[:], AX.X, ALU.add).then_inc(coef_ready, 1)

            def pre_from_pe(c):
                eng.wait_ge(xfp_done, c + 1)
                n = NBLK // 2
                done(nc.vector.tensor_tensor(xf_p[:], xfp_ps[:, 0:n * NS].rearrange("p (n j) -> p n j", j=NS),
                                             over(jmask.unsqueeze(1), [P, n, NS]), ALU.mult))
                nc.vector.tensor_reduce(coef_p[:, n * c:n * (c + 1)], xf_p[:], AX.X, ALU.add).then_inc(pre_ready, 1)

            squares(0)
            arguments(0)
            start(0)
            iterate((0,), PLAN[0])
            squares(1)
            iterate((0,), PLAN[1])
            arguments(1)
            iterate((0,), PLAN[2])
            start(1)
            iterate((0, 1), PLAN[3])
            squares(2)
            iterate((0, 1), PLAN[4])
            arguments(2)
            iterate((0, 1), PLAN[5])
            start(2)
            iterate((0, 1), PLAN[6])
            pre_from_pe(0)
            squares(3)
            iterate((0, 1), PLAN[7])
            arguments(3)
            iterate((0, 1), left[0])
            start(3)
            res_to_pe(0)
            iterate((1, 2, 3), 1)
            res_from_pe(0)
            iterate((1, 2, 3), PLAN[8])
            pre_from_pe(1)
            iterate((1, 2, 3), left[1])
            res_to_pe(1)
            iterate((2, 3), 1)
            res_from_pe(1)
            iterate((2, 3), left[2] - PLAN[9])
            eng.sem_inc(sink_near, 1)
            iterate((2, 3), left[2])
            res_to_pe(2)
            res_to_pe(3)
            res_from_pe(2)
            res_from_pe(3)

            def end_out(u, slot):
                for bp in range(2):
                    eng.wait_ge(end_done, 2 * u + bp + 1)
                    pu = part[:, ds(u, 1)].rearrange("p u b c -> p (u b) c")[:, 2 * bp:2 * bp + 2, :]
                    nc.vector.tensor_tensor(pu, mix_ps[slot][bp][:, :].rearrange("p (b c) -> p b c", b=2), pu,
                                            ALU.add).then_inc(end_read, 1)

            eng.wait_ge(x_added, NU)
            with eng.Fori(0, HU // 2) as i:
                for slot in range(2):
                    end_out(2 * i + slot, slot)


_OUT_SHAPE = (32, 64, 1024)


def kernel(x, cond_128, fside_S_0, L0_cond_weight, L0_cond_c_weight, L0_ffn_W_res, L0_ffn_W_pre, L0_ffn_W_post,
           L0_ffn_H_res_base, L0_ffn_H_pre_base, L0_ffn_H_post_base, L0_ffn_gate, L0_ffn_W_branch):
    import concourse.bacc as _bacc
    from concourse import mybir as _mybir
    from concourse.bass_utils import run_bass_kernel_spmd as _run

    x = np.ascontiguousarray(x)
    cw = np.asarray(L0_cond_weight)
    co_n, gi, taps = cw.shape
    conv_w = np.zeros((3, 32, 2, 3, 32), cw.dtype)
    for half in range(2):
        for g in range(2):
            blk = cw[32 * half + 16 * g:32 * half + 16 * (g + 1)].reshape(16, 16, 3, 3)
            conv_w[:, 16 * g:16 * (g + 1), half, :, 16 * g:16 * (g + 1)] = blk.transpose(3, 1, 2, 0)
    conv_w = conv_w.reshape(96, 2, 3, 32)
    ctx_w = np.ascontiguousarray(np.tile(np.asarray(L0_cond_c_weight).T.reshape(128, 2, 1, 32), (1, 1, 4, 1))
                                 .reshape(128, 2, 128))
    cond_t = np.ascontiguousarray(np.asarray(cond_128).T)
    bias_c = np.ascontiguousarray(np.tile(np.asarray(fside_S_0).reshape(2, 32), (1, 4)).T)
    w_all = np.concatenate([np.asarray(L0_ffn_W_res), np.asarray(L0_ffn_W_pre), np.asarray(L0_ffn_W_post)], axis=0)
    proj_w = np.zeros((128, 2, 4, 32), w_all.dtype)
    proj_w[:, :, :, 0:24] = w_all.reshape(24, 4, 2, 128).transpose(3, 2, 1, 0)
    branch_w = np.ascontiguousarray(np.asarray(L0_ffn_W_branch).reshape(2, 128, 256).transpose(1, 0, 2))
    base = np.concatenate([np.asarray(L0_ffn_H_res_base).reshape(-1), np.asarray(L0_ffn_H_pre_base),
                           np.asarray(L0_ffn_H_post_base)])
    base = np.ascontiguousarray(np.broadcast_to(base[None], (128, 24)))
    gate = np.ascontiguousarray(np.broadcast_to(np.asarray(L0_ffn_gate).reshape(1, 1), (128, 1)))
    consts = np.zeros((128, 2 * 128 + 8 + 24 + 16), np.float32)
    consts[:, 0:128] = np.eye(128)
    consts[:, 128:256] = np.tile(np.eye(32), (4, 4))
    consts[:, 256:260] = np.repeat(np.eye(4), 32, axis=0)
    consts[:, 264:288] = np.tile(np.eye(32)[:, 0:24], (4, 1))
    consts[:, 288:304] = np.eye(4).reshape(1, 16)

    nc = _bacc.Bacc("TRN2", target_bir_lowering=False, num_devices=1)
    f32 = _mybir.dt.float32
    feeds, args = {}, []
    for name, a in (("x", x), ("conv_w", conv_w), ("ctx_w", ctx_w), ("cond_t", cond_t), ("bias_c", bias_c),
                    ("proj_w", proj_w), ("branch_w", branch_w), ("base", base), ("gate", gate), ("consts", consts)):
        feeds[f"in_{name}"] = a
        args.append(nc.dram_tensor(f"in_{name}", a.shape, f32, kind="ExternalInput").ap())
    out = nc.dram_tensor("out_0", _OUT_SHAPE, f32, kind="ExternalOutput").ap()
    adaln_ffn_program(nc, args[0], out, *args[1:])
    r = _run(nc, [feeds], core_ids=[0])
    return r.results[0]["out_0"]
```

```python
import numpy as np


def adaln_ffn_program(nc, x, out, conv_w, ctx_w, cond_t, bias_c, proj_w, branch_w, base, gate, consts):
    import concourse.bass as bass
    from concourse import mybir
    from contextlib import ExitStack

    f32 = mybir.dt.float32
    ALU = mybir.AluOpType
    ACT = mybir.ActivationFunctionType
    AX = mybir.AxisListType
    ds = bass.ds

    N, CH, L = x.shape
    P = 128
    BT = 32
    NS = 4
    C = L // NS
    NBLK = N * CH // BT
    UB = 4
    NU = NBLK // UB
    QU = 4
    NQ = NU // QU
    HU = NU // 2
    TS, TQ = 3, 3
    PAD = 4
    XW = L + 2 * PAD - TS + 1
    NE = NS * NS + 2 * NS
    HH = NS * NS
    SINK_ITERS = 50
    ITER_BODY = 12
    AHEAD = 4
    SPREAD_AT = 2
    PLAN = [16, 3, 11, 2, 2, 1, 2]
    WARM_START, WARM_END, WARM_GAP = 4, 4, 3
    TAU_INV = 10.0
    RMS_EPS = 1.1920929e-07
    BIG = float(2.0 ** 120)
    LN_BIG = float(120.0 * np.log(2.0))
    CLAMP = -8.0

    with ExitStack() as ctx:
        def sb(name, shape):
            return ctx.enter_context(nc.sbuf_tensor(name, shape, f32))

        def pb(name):
            return ctx.enter_context(nc.psum_tensor(name, [P, 512], f32))

        def sem(name):
            return ctx.enter_context(nc.semaphore(name))

        cst = sb("cst", [P, P + BT + NE + HH])
        ident = cst[:, 0:P]
        lane = cst[:, P:P + BT]
        select = cst[:, P + BT:P + BT + NE]
        eye4 = cst[:, P + BT + NE:P + BT + NE + HH]
        convw = sb("convw", [TS * BT, 2, TQ, BT])
        projw = sb("projw", [P, 2, NS, BT])
        branchw = sb("branchw", [P, 2, C])
        ctxw = sb("ctxw", [P, 2, P])
        condt = sb("condt", [P, N])
        biasc = sb("biasc", [P, 2])
        base_s = sb("base_s", [P, NE])
        gate_s = sb("gate_s", [P, 1])
        bias_all = sb("bias_all", [P, NBLK])
        g_s = sb("g_s", [P, 4])
        g_eye = sb("g_eye", [P, HH])
        lnbig = sb("lnbig", [P, 1])
        eps = sb("eps", [P, 1])

        xin_all = sb("xin", [P, QU * UB * XW])
        xin = xin_all[0:TS * BT, :].rearrange("p (k b w) -> p k b w", k=QU, b=UB)
        part = xin_all[:, 0:HU * UB * C].rearrange("p (u b c) -> p u b c", u=HU, b=UB)
        h_now = sb("h_now", [P, 2, UB, C])
        h_all = sb("h_all", [P, NBLK, C])
        ht_y = sb("ht_y", [P, 2 * QU * 512])
        ht = ht_y[:, :].rearrange("p (a k n) -> p a k n", a=2, k=QU)
        y_all = ht_y[:, :].rearrange("p (u c) -> p u c", u=NU)
        sq_junk = sb("sq_junk", [P, 2, C])
        zeros = sb("zeros", [P, 512])
        ssq = sb("ssq", [P, NBLK])
        lp_s = sb("lp_s", [P, 512])
        raw_l = sb("raw_l", [P, NU, NE])
        ssq_q = sb("ssq_q", [P, QU * UB])
        rt = sb("rt", [P, NU])

        inv = sb("inv", [P, QU])
        lg = sb("lg", [P, QU, NE])
        la = sb("la", [P, QU, NE])
        gmax = sb("gmax", [P, QU * NE // NS])
        colmax = sb("colmax", [P, QU, NS])
        zb = sb("zb", [P, NS, QU, NS])
        zc = sb("zc", [P, NS, QU, NS])
        e_h = sb("e_h", [P, QU, HH])
        e_p = sb("e_p", [P, QU, 2 * NS])
        p_a = sb("p_a", [P, NS, QU, NS])
        p_b = sb("p_b", [P, NS, QU, NS])
        s_a = sb("s_a", [P, NS, QU])
        r_a = sb("r_a", [P, NS, QU])
        s_c = sb("s_c", [P, QU * NS])
        r_c = sb("r_c", [P, QU * NS])
        s_p = sb("s_p", [P, 2 * QU])
        r_p = sb("r_p", [P, 2 * QU])
        soft = sb("soft", [P, NU, 2 * NS])
        holds = {"0": (0,), "1": (1,), "2": (2,), "3": (3,), "0a": (0,), "0b": (0,), "01": (0, 1), "23": (2, 3)}
        sk_n = {st: QU // 2 if st in ("0a", "0b") else QU * len(quads) for st, quads in holds.items()}
        sk = {st: sb(f"sk_{st}", [P, NS, n, NS]) for st, n in sk_n.items()}
        sk_s = {st: sb(f"sum_{st}", [P, NS * n]) for st, n in sk_n.items()}
        sk_r = {st: sb(f"rec_{st}", [P, NS * n]) for st, n in sk_n.items()}
        hk = sb("hk", [P, QU, HH])
        coef = sb("coef", [P, NBLK, NS])
        coef_p = sb("coef_p", [P, NBLK])

        pre_m = sb("pre_m", [P, 2, UB, BT])
        res_m = sb("res_m", [P, 2, UB, NS, BT])
        post_m = sb("post_m", [P, 2, UB, NS, BT])
        xp_s = sb("xp_s", [P, 2, C])
        xpt_s = sb("xpt_s", [P, 2, C])
        xres = sb("xres", [P, 2, UB, C])
        ost = h_now

        banks = [pb(f"bank{i}") for i in range(8)]
        conv_ps = [banks[0], banks[1]]
        ht_ps = [banks[2], banks[3]]
        lp_ps = banks[4]
        sel_ps = banks[5]
        xp_ps, xpt_ps, y_ps = banks[2], banks[3], banks[4]
        mix_ps = [[banks[0], banks[1]], [banks[6], banks[7]]]
        xfp_ps, xfh_ps = banks[2], banks[5]

        convw_loaded = sem("convw_loaded")
        zeros_ready = sem("zeros_ready")
        sink_near = sem("sink_near")
        ctx_loaded = sem("ctx_loaded")
        w_loaded = sem("w_loaded")
        x_margin = sem("x_margin")
        x_first = sem("x_first")
        x_loaded = [sem(f"x_loaded{k}") for k in range(QU)]
        conv_done = sem("conv_done")
        h_ready = sem("h_ready")
        conv_read = sem("conv_read")
        h_kept = sem("h_kept")
        t_done = sem("t_done")
        ht_ready = sem("ht_ready")
        logit_done = sem("logit_done")
        lp_ready = sem("lp_ready")
        sel_done = sem("sel_done")
        ctx_done = sem("ctx_done")
        bias_ready = sem("bias_ready")
        gexp = sem("gexp")
        dve = sem("dve")
        sink = sem("sink")
        rt_ready = sem("rt_ready")
        args_ready = sem("args_ready")
        exps_ready = sem("exps_ready")
        soft_ready = sem("soft_ready")
        hk_ready = sem("hk_ready")
        xfp_done = sem("xfp_done")
        xfh_done = sem("xfh_done")
        pre_ready = sem("pre_ready")
        coef_ready = sem("coef_ready")
        pre_built = sem("pre_built")
        xp_done = sem("xp_done")
        xp_ready = sem("xp_ready")
        xpt_done = sem("xpt_done")
        xpt_ready = sem("xpt_ready")
        y_done = sem("y_done")
        y_ready = sem("y_ready")
        post_built = sem("post_built")
        res_built = sem("res_built")
        mix_done = sem("mix_done")
        mix_read = sem("mix_read")
        x_added = sem("x_added")
        end_done = sem("end_done")
        end_read = sem("end_read")
        r_loaded = [sem(f"r_loaded{k}") for k in range(2)]
        end_stored = sem("end_stored")
        stored = [sem(f"stored{k}") for k in range(2)]

        W_LOADS = 4


        x_cv = x.rearrange("n (h c) l -> c (n h) l", h=2)
        x_tok = x.rearrange("n (h c) (j l) -> j c (n h) l", h=2, j=NS)
        o_tok = out.rearrange("n (h c) (j l) -> j c (n h) l", h=2, j=NS)

        def store_end(queue, streams):
            with queue.Fori(0, HU // 2) as i:
                queue.wait_ge(end_read, 4 * i + 4)
                for j in streams:
                    queue.dma_start(o_tok[j, :, ds(HU * UB + 2 * UB * i, 2 * UB), :],
                                    part[BT * j:BT * (j + 1), ds(2 * i, 2)].rearrange("p u b c -> p (u b) c")
                                    ).then_inc(end_stored, 16)

        block = ctx.enter_context(nc.Block())

        @block.sync
        def _(sp):
            def load_unit(u, k):
                for s in range(TS):
                    sp.dma_start(xin[BT * s:BT * (s + 1), k, :, PAD - s:PAD - s + L],
                                 x_cv[:, ds(UB * u, UB), :]).then_inc(x_loaded[k], 16)

            def load_res(u, slot):
                for j in range(NS):
                    sp.dma_start(xres[BT * j:BT * (j + 1), slot, :, :],
                                 x_tok[j, :, ds(UB * u, UB), :]).then_inc(r_loaded[slot], 16)

            def store(u, tile, slot):
                for j in range(NS):
                    sp.dma_start(o_tok[j, :, ds(UB * u, UB), :],
                                 tile[BT * j:BT * (j + 1), :, :]).then_inc(stored[slot], 16)

            sp.wait_ge(x_margin, 1)
            for half, signal in ((0, x_first), (1, x_loaded[0])):
                for s in range(TS):
                    sp.dma_start(xin[BT * s:BT * (s + 1), 0, half::2, PAD - s:PAD - s + L],
                                 x_cv[:, half:UB:2, :]).then_inc(signal, 16)
            for k in range(1, QU):
                load_unit(k, k)
            with sp.Fori(1, NQ) as i:
                for k in range(QU):
                    sp.wait_ge(conv_done, 2 * QU * i + 2 * (k + 1 - QU))
                    load_unit(QU * i + k, k)
            for slot in range(2):
                load_res(HU + slot, slot)
            with sp.Fori(0, HU // 2 - 1) as i:
                for slot in range(2):
                    sp.wait_ge(x_added, 2 * i + slot + 1)
                    load_res(HU + 2 * i + slot + 2, slot)
            for slot in range(2):
                sp.wait_ge(x_added, HU - 1 + slot)
                load_res(slot, slot)
            with sp.Fori(0, HU // 2 - 1) as i:
                for slot in range(2):
                    sp.wait_ge(x_added, 2 * i + slot + HU + 1)
                    store(2 * i + slot, ost[:, slot], slot)
                    load_res(2 * i + slot + 2, slot)
            for slot in range(2):
                sp.wait_ge(x_added, NU - 1 + slot)
                store(HU - 2 + slot, ost[:, slot], slot)
            store_end(sp, (0, 1))
            for slot in range(2):
                sp.wait_ge(stored[slot], 16 * NS * HU // 2)
            sp.wait_ge(end_stored, 16 * NS * HU // 2)

        @block.tensor
        def _(pe):
            def conv(u, k, i, half, first=False):
                if first and k == 0 and half == 0:
                    pe.wait_ge(x_first, 16 * TS)
                elif half == 0 or (first and k == 0):
                    pe.wait_ge(x_loaded[k], 16 * TS * (i + 1))
                if not first:
                    pe.wait_ge(conv_read, 2 * u + half - 1)
                for q in range(TQ):
                    for j in range(NS):
                        last = nc.tensor.matmul(conv_ps[half][BT * j:BT * (j + 1), :].rearrange("p (b c) -> p b c", b=2),
                                                convw[:, half, q, :],
                                                xin[:, k, half::2, C * j + TS * q:C * j + TS * q + C],
                                                start=(q == 0), stop=(q == TQ - 1))
                last.then_inc(conv_done, 1)

            def transpose_h(u, slot, first=False):
                pe.wait_ge(h_ready, 2 * u + 2)
                for a in range(2):
                    if not first:
                        pe.wait_ge(ht_ready, 2 * u + a - 1)
                    for b in range(UB):
                        last = nc.tensor.transpose(ht_ps[a][:, P * b:P * (b + 1)],
                                                   h_now[:, slot, b, P * a:P * (a + 1)], ident)
                    last.then_inc(t_done, 1)

            def logits(i):
                pe.wait_ge(ht_ready, 2 * QU * (i + 1))
                for a in range(2):
                    hv = ht[:, a].rearrange("p k (b j t) -> p (k b) j t", b=UB, j=NS)
                    for j in range(NS):
                        last = nc.tensor.matmul(lp_ps[BT * j:BT * (j + 1), :], projw[:, a, j, :], hv[:, :, j, :],
                                                start=(a == 0), stop=(a == 1))
                last.then_inc(logit_done, 1)

            def to_tokens(i):
                pe.wait_ge(lp_ready, i + 1)
                for k in range(QU):
                    nc.tensor.matmul(sel_ps[:, NE * k:NE * (k + 1)], lp_s[:, P * k:P * (k + 1)], select,
                                     start=True, stop=True)
                for b in range(UB):
                    last = nc.tensor.matmul(sel_ps[BT * b:BT * (b + 1), NE * QU:NE * QU + QU], lane,
                                            ssq_q[:, b::UB], start=True, stop=True)
                last.then_inc(sel_done, 1)

            def keep_warm(n):
                for m in range(n):
                    nc.tensor.matmul(banks[3][:, :], zeros[:, 0:P], zeros[:, :], start=True, stop=True)

            def context():
                pe.wait_ge(ctx_loaded, 16 * 4)
                for half in range(2):
                    last = nc.tensor.matmul(sel_ps[:, N * half:N * (half + 1)], ctxw[:, half, :], condt[:],
                                            start=True, stop=True)
                last.then_inc(ctx_done, 1)

            def quad(i, first):
                u = QU * i
                conv(u, 0, i, 0, first=first)
                if first:
                    context()
                else:
                    transpose_h(u - 1, 1)
                conv(u, 0, i, 1, first=first)
                if not first:
                    logits(i - 1)
                conv(u + 1, 1, i, 0)
                if not first:
                    to_tokens(i - 1)
                conv(u + 1, 1, i, 1)
                if first:
                    pe.wait_ge(w_loaded, 16 * W_LOADS)
                transpose_h(u, 0, first=first)
                for k in (2, 3):
                    conv(u + k, k, i, 0)
                    conv(u + k, k, i, 1)
                    transpose_h(u + k - 1, (k - 1) % 2)

            def x_pre(u, slot, first=False):
                pe.wait_ge(pre_built, u + 1)
                if not first:
                    pe.wait_ge(xp_ready, u)
                for b in range(UB):
                    last = nc.tensor.matmul(xp_ps[BT * b:BT * (b + 1), 0:C], pre_m[:, slot, b, :],
                                            h_all[:, UB * u + b, :], start=True, stop=True)
                last.then_inc(xp_done, 1)

            def x_pre_t(u, slot, first=False):
                pe.wait_ge(xp_ready, u + 1)
                if not first:
                    pe.wait_ge(xpt_ready, u)
                for a in range(2):
                    last = nc.tensor.transpose(xpt_ps[:, P * a:P * (a + 1)],
                                               xp_s[:, slot, P * a:P * (a + 1)], ident)
                last.then_inc(xpt_done, 1)

            def branch(u, slot, first=False):
                pe.wait_ge(xpt_ready, u + 1)
                if not first:
                    pe.wait_ge(y_ready, u)
                for a in range(2):
                    last = nc.tensor.matmul(y_ps[:, 0:C], xpt_s[:, slot, P * a:P * (a + 1)],
                                            branchw[:, a, :], start=(a == 0), stop=(a == 1))
                last.then_inc(y_done, 1)

            def branch_half(c):
                for t in range(HU * c, HU * (c + 1) + 2):
                    if t < HU * (c + 1):
                        x_pre(t, t % 2, t == 0)
                    if HU * c <= t - 1 < HU * (c + 1):
                        x_pre_t(t - 1, (t - 1) % 2, t - 1 == 0)
                    if t - 2 >= HU * c:
                        branch(t - 2, t % 2, t - 2 == 0)

            def mix(m, u, slot, res, first=False):
                pe.wait_ge(post_built, m + 1)
                if res:
                    pe.wait_ge(res_built, u + 1)
                pe.wait_ge(y_ready, u + 1)
                for bp in range(2):
                    if not first:
                        pe.wait_ge(mix_read, 2 * m + bp - 3)
                    for b in (2 * bp, 2 * bp + 1):
                        o = mix_ps[slot][bp][:, C * (b % 2):C * (b % 2 + 1)]
                        if res:
                            nc.tensor.matmul(o, res_m[:, slot, b], h_all[:, ds(UB * u + b, 1), :],
                                             start=True, stop=False)
                        last = nc.tensor.matmul(o, post_m[:, slot, b], y_all[:, ds(u, 1), :],
                                                start=not res, stop=True)
                    last.then_inc(mix_done, 1)

            def end(u, slot, first=False):
                pe.wait_ge(res_built, u + HU + 1)
                for bp in range(2):
                    if not first:
                        pe.wait_ge(end_read, 2 * u + bp - 3)
                    for b in (2 * bp, 2 * bp + 1):
                        last = nc.tensor.matmul(mix_ps[slot][bp][:, C * (b % 2):C * (b % 2 + 1)], res_m[:, slot, b],
                                                h_all[:, ds(UB * (u + HU) + b, 1), :], start=True, stop=True)
                    last.then_inc(end_done, 1)

            def spread(dst, src):
                for b in range(UB):
                    for j in range(NS):
                        last = nc.tensor.matmul(dst(j, b), ident[:, BT * b:BT * (b + 1)], src(j), start=True, stop=True)
                return last

            def spread_pre(c):
                pe.wait_ge(soft_ready, 2 * (c + 1))
                spread(lambda j, b: xfp_ps[BT * j:BT * (j + 1), b:HU * UB:UB],
                       lambda j: soft[:, HU * c:HU * (c + 1), j]).then_inc(xfp_done, 1)

            def spread_res(q):
                pe.wait_ge(hk_ready, q + 1)
                if q:
                    pe.wait_ge(coef_ready, q)
                spread(lambda j, b: xfh_ps[BT * j:BT * (j + 1), 0:QU * UB * NS]
                       .rearrange("p (u b i) -> p b u i", u=QU, b=UB)[:, b],
                       lambda j: hk[:].rearrange("p u (i j) -> p j u i", j=NS)[:, j]).then_inc(xfh_done, 1)

            pe.wait_ge(zeros_ready, 1)
            keep_warm(WARM_START)
            pe.wait_ge(convw_loaded, 16)
            quad(0, True)
            with pe.Fori(1, NQ) as i:
                quad(i, False)
            transpose_h(NU - 1, 1)
            logits(NQ - 1)
            to_tokens(NQ - 1)
            spread_pre(0)
            branch_half(0)
            spread_pre(1)
            branch_half(1)
            spread_res(0)
            for slot in range(2):
                mix(slot, HU + slot, slot, False, first=True)
            with pe.Fori(1, HU // 2) as i:
                for slot in range(2):
                    mix(2 * i + slot, HU + 2 * i + slot, slot, False)
            for u in range(QU):
                if u == QU - 1:
                    spread_res(1)
                mix(HU + u, u, u % 2, True)
            with pe.Fori(QU // 2, HU // 2) as i:
                for slot in range(2):
                    mix(HU + 2 * i + slot, 2 * i + slot, slot, True)
            pe.wait_ge(mix_read, 2 * NU)
            pe.wait_ge(sink_near, 1)
            keep_warm(WARM_END)
            spread_res(2)
            keep_warm(WARM_GAP)
            for u in range(QU):
                end(u, u % 2, first=u < 2)
                if u == SPREAD_AT:
                    spread_res(3)
            with pe.Fori(QU // 2, HU // 2) as i:
                for slot in range(2):
                    end(2 * i + slot, slot)

        @block.scalar
        def _(act):
            def conv_out(u, slot, half, first=False):
                if half == 0 and not first:
                    act.wait_ge(t_done, 2 * u - 2)
                    act.wait_ge(h_kept, u - 1)
                act.wait_ge(conv_done, 2 * u + half + 1)
                for n in range(2):
                    b = 2 * n + half
                    last = nc.scalar.activation(h_now[:, slot, b, :], conv_ps[half][:, C * n:C * (n + 1)], ACT.Identity,
                                                bias=bias_all[:, ds(UB * u + b, 1)])
                last.then_inc(h_ready, 1)
                if not first or half or slot:
                    act.wait_ge(conv_read, 2 * u + half)
                for n in range(2):
                    b = UB * u + 2 * n + half
                    last = nc.scalar.activation(sq_junk[:, n, :], conv_ps[half][:, C * n:C * (n + 1)], ACT.Square,
                                                bias=bias_all[:, ds(b, 1)], accum_out=ssq[:, ds(b, 1)])
                last.then_inc(conv_read, 1)

            def ht_out(u, k, i, first=False):
                for a in range(2):
                    act.wait_ge(t_done, 2 * u + a + 1)
                    if not first:
                        act.wait_ge(logit_done, i)
                    nc.scalar.copy(ht[:, a, k, :], ht_ps[a][:, :]).then_inc(ht_ready, 1)

            def logits_out(i, first=False):
                act.wait_ge(logit_done, i + 1)
                if not first:
                    act.wait_ge(sel_done, i)
                nc.scalar.copy(ssq_q[:], ssq[:, ds(QU * UB * i, QU * UB)])
                nc.scalar.copy(lp_s[:], lp_ps[:, :]).then_inc(lp_ready, 1)

            def tokens_out(i):
                act.wait_ge(sel_done, i + 1)
                nc.scalar.copy(raw_l[:, ds(QU * i, QU), :],
                               sel_ps[:, 0:NE * QU].rearrange("p (k e) -> p k e", e=NE))
                nc.scalar.activation(rt[:, ds(QU * i, QU)], sel_ps[:, NE * QU:NE * QU + QU], ACT.Sqrt, scale=1.0 / L,
                                     bias=eps[:, 0:1]).then_inc(rt_ready, 1)

            def exponentials(c):
                act.wait_ge(args_ready, c + 1)
                nc.scalar.activation(e_h[:], la[:, :, 0:HH], ACT.Exp, scale=TAU_INV)
                nc.scalar.activation(e_p[:], la[:, :, HH:NE], ACT.Exp)
                nc.scalar.activation(p_a[:], zb[:], ACT.Exp, scale=TAU_INV)
                nc.scalar.activation(p_b[:], zc[:], ACT.Exp, scale=TAU_INV, bias=lnbig[:, 0:1]).then_inc(exps_ready, 1)

            def quad(i, last_quad, early=False):
                u = QU * i
                first = last_quad is None
                conv_out(u, 0, 0, first)
                if last_quad:
                    ht_out(u - 1, 3, i - 1, *last_quad)
                conv_out(u, 0, 1, first)
                if last_quad:
                    logits_out(i - 1, *last_quad)
                conv_out(u + 1, 1, 0, first)
                if last_quad:
                    tokens_out(i - 1)
                conv_out(u + 1, 1, 1, first)
                if early:
                    exponentials(i - 1)
                ht_out(u, 0, i, first)
                conv_out(u + 2, 0, 0)
                if last_quad and not early:
                    exponentials(i - 1)
                conv_out(u + 2, 0, 1)
                ht_out(u + 1, 1, i, first)
                conv_out(u + 3, 1, 0)
                conv_out(u + 3, 1, 1)
                ht_out(u + 2, 2, i, first)

            def x_pre_out(u, slot, first=False):
                act.wait_ge(xp_done, u + 1)
                if not first:
                    act.wait_ge(xpt_done, u - 1)
                nc.scalar.copy(xp_s[:, slot, :], xp_ps[:, 0:C]).then_inc(xp_ready, 1)

            def x_pre_t_out(u, slot, first=False):
                act.wait_ge(xpt_done, u + 1)
                if not first:
                    act.wait_ge(y_done, u - 1)
                nc.scalar.copy(xpt_s[:, slot, :], xpt_ps[:, 0:C]).then_inc(xpt_ready, 1)

            def branch_out(u, slot):
                act.wait_ge(y_done, u + 1)
                nc.scalar.copy(y_all[:, ds(u, 1), :], y_ps[:, 0:C]).then_inc(y_ready, 1)

            def branch_half(c):
                u = HU * c
                x_pre_out(u, 0, c == 0)
                x_pre_out(u + 1, 1, c == 0)
                x_pre_t_out(u, 0, c == 0)
                x_pre_out(u + 2, 0)
                x_pre_t_out(u + 1, 1, c == 0)
                branch_out(u, 0)
                with act.Fori(u // 2 + 1, (u + HU) // 2 - 1) as i:
                    for slot in range(2):
                        x_pre_out(2 * i + slot + 1, 1 - slot)
                        x_pre_t_out(2 * i + slot, slot)
                        branch_out(2 * i + slot - 1, 1 - slot)
                x_pre_out(u + HU - 1, 1)
                x_pre_t_out(u + HU - 2, 0)
                branch_out(u + HU - 3, 1)
                x_pre_t_out(u + HU - 1, 1)
                branch_out(u + HU - 2, 0)
                branch_out(u + HU - 1, 1)

            def pre_out(c):
                act.wait_ge(xfp_done, c + 1)
                n = NBLK // 2
                nc.scalar.copy(coef_p[:, n * c:n * (c + 1)], xfp_ps[:, 0:n]).then_inc(pre_ready, 1)

            def res_out(q):
                act.wait_ge(xfh_done, q + 1)
                n = QU * UB
                nc.scalar.copy(coef[:, n * q:n * (q + 1), :], xfh_ps[:, 0:n * NS].rearrange("p (b i) -> p b i", i=NS)
                               ).then_inc(coef_ready, 1)

            def mix_out(m, slot, tile):
                for bp in range(2):
                    act.wait_ge(mix_done, 2 * m + bp + 1)
                    nc.scalar.copy(tile(bp), mix_ps[slot][bp][:, :].rearrange("p (b c) -> p b c", b=2)
                                   ).then_inc(mix_read, 1)

            def to_ost(slot):
                return lambda bp: ost[:, slot, 2 * bp:2 * bp + 2, :]

            for dst, src in ((convw, conv_w),):
                act.dma_start(dst[:], src).then_inc(convw_loaded, 16)
            for dst, src in ((ctxw, ctx_w), (condt, cond_t), (biasc, bias_c), (gate_s, gate)):
                act.dma_start(dst[:], src).then_inc(ctx_loaded, 16)
            for dst, src in ((cst, consts), (projw, proj_w), (base_s, base), (branchw, branch_w)):
                act.dma_start(dst[:], src).then_inc(w_loaded, 16)
            act.wait_ge(ctx_loaded, 16 * 4)
            nc.scalar.activation(g_s[:, 0:1], gate_s[:], ACT.Exp, scale=-1.0).then_inc(gexp, 1)
            act.wait_ge(bias_ready, 1)
            quad(0, None)
            quad(1, (True,), early=True)
            with act.Fori(2, NQ) as i:
                quad(i, (False,))
            ht_out(NU - 1, 3, NQ - 1)
            logits_out(NQ - 1)
            tokens_out(NQ - 1)
            pre_out(0)
            exponentials(NQ - 1)
            branch_half(0)
            pre_out(1)
            branch_half(1)
            res_out(0)
            with act.Fori(0, HU // 2) as i:
                for slot in range(2):
                    pu = part[:, ds(2 * i + slot, 1)].rearrange("p u b c -> p (u b) c")
                    mix_out(2 * i + slot, slot, lambda bp: pu[:, 2 * bp:2 * bp + 2, :])
            act.wait_ge(h_kept, NU)
            for u in range(QU):
                if u >= 2:
                    act.wait_ge(stored[u % 2], 16 * NS)
                if u == QU - 1:
                    res_out(1)
                mix_out(HU + u, u % 2, to_ost(u % 2))
            with act.Fori(QU // 2, HU // 2) as i:
                for slot in range(2):
                    act.wait_ge(stored[slot], 16 * NS * i)
                    mix_out(HU + 2 * i + slot, slot, to_ost(slot))
            res_out(2)
            res_out(3)
            store_end(act, (2, 3))

        @block.gpsimd
        def _(pool):
            nc.gpsimd.memset(xin[:, :, :, 0:PAD], 0.0)
            nc.gpsimd.memset(xin[:, :, :, XW - PAD:XW], 0.0).then_inc(x_margin, 1)
            nc.gpsimd.memset(eps[:], RMS_EPS)
            nc.gpsimd.memset(lnbig[:], LN_BIG).then_inc(x_margin, 1)

            with pool.Fori(0, NU // 2) as i:
                for slot in range(2):
                    pool.wait_ge(h_ready, 4 * i + 2 * slot + 2)
                    nc.gpsimd.tensor_copy(h_all[:, ds(UB * (2 * i + slot), UB), :], h_now[:, slot]).then_inc(h_kept, 1)

            def build_pre(u, slot, first=False):
                if not first:
                    pool.wait_ge(xp_done, u - 1)
                nc.gpsimd.tensor_tensor(pre_m[:, slot], lane.unsqueeze(1).to_broadcast([P, UB, BT]),
                                        coef_p[:, ds(UB * u, UB)].unsqueeze(2).to_broadcast([P, UB, BT]),
                                        ALU.mult).then_inc(pre_built, 1)

            def build_post(m, u, slot, first=False):
                if not first:
                    pool.wait_ge(mix_done, 2 * m - 2)
                nc.gpsimd.tensor_tensor(
                    post_m[:, slot],
                    ident.rearrange("p (b t) -> p b t", b=UB).unsqueeze(2).to_broadcast([P, UB, NS, BT]),
                    soft[:, ds(u, 1), NS:2 * NS].rearrange("p u i -> p (u i)").unsqueeze(1).unsqueeze(3)
                    .to_broadcast([P, UB, NS, BT]),
                    ALU.mult).then_inc(post_built, 1)

            def build_res(u, slot, used=None):
                if used is not None:
                    pool.wait_ge(*used)
                nc.gpsimd.tensor_tensor(
                    res_m[:, slot].rearrange("p b i t -> p (b i) t"),
                    lane.unsqueeze(1).to_broadcast([P, UB * NS, BT]),
                    coef[:, ds(UB * u, UB), :].rearrange("p b i -> p (b i)").unsqueeze(2).to_broadcast([P, UB * NS, BT]),
                    ALU.mult).then_inc(res_built, 1)

            def add_x(m, slot, tile):
                pool.wait_ge(mix_read, 2 * m + 2)
                pool.wait_ge(r_loaded[slot], 8 * NS * (m - slot) + 16 * NS)
                nc.gpsimd.tensor_tensor(tile, tile, xres[:, slot], ALU.add).then_inc(x_added, 1)

            def of_part(m):
                return part[:, ds(m, 1)].rearrange("p u b c -> p (u b) c")

            pool.wait_ge(pre_ready, 1)
            for slot in range(2):
                build_pre(slot, slot, True)
            with pool.Fori(1, HU // 2) as i:
                for slot in range(2):
                    build_pre(2 * i + slot, slot)
            pool.wait_ge(pre_ready, 2)
            with pool.Fori(HU // 2, NU // 2) as i:
                for slot in range(2):
                    build_pre(2 * i + slot, slot)
            for slot in range(2):
                build_post(slot, HU + slot, slot, True)
            pool.wait_ge(coef_ready, 1)
            for slot in range(2):
                build_res(slot, slot)
            with pool.Fori(0, HU // 2 - 1) as i:
                for slot in range(2):
                    add_x(2 * i + slot, slot, of_part(2 * i + slot))
                    build_post(2 * i + slot + 2, HU + 2 * i + slot + 2, slot)
            for slot in range(2):
                add_x(HU - 2 + slot, slot, of_part(HU - 2 + slot))
                build_post(HU + slot, slot, slot)
            for u in range(HU):
                add_x(HU + u, u % 2, ost[:, u % 2])
                if u + 2 == QU:
                    pool.wait_ge(coef_ready, 2)
                if u + 2 < HU:
                    build_post(HU + u + 2, u + 2, u % 2)
                    build_res(u + 2, u % 2)
            pool.wait_ge(coef_ready, 3)
            for slot in range(2):
                build_res(HU + slot, slot)
            for u in range(2, QU):
                build_res(HU + u, u % 2, (end_done, 2 * u - 2))
            pool.wait_ge(coef_ready, 4)
            with pool.Fori((HU + QU) // 2, NU // 2) as i:
                for slot in range(2):
                    build_res(2 * i + slot, slot, (end_done, 4 * i + 2 * slot - 2 * HU - 2))

        @block.vector
        def _(eng):
            steps = [0]

            def step(ins):
                steps[0] += 1
                ins.then_inc(dve, 1)
                return steps[0]

            def need(count):
                eng.wait_ge(dve, count)

            def done(ins):
                need(step(ins))

            def over(ap, shape):
                return ap.to_broadcast(shape)

            nc.vector.memset(zeros[:], 0.0).then_inc(zeros_ready, 1)
            eng.wait_ge(ctx_done, 1)
            eng.wait_ge(gexp, 1)
            eng.wait_ge(w_loaded, 16 * W_LOADS)
            for half in range(2):
                last = nc.vector.tensor_scalar(bias_all[:].rearrange("p (n h) -> p n h", h=2)[:, :, half],
                                               sel_ps[:, N * half:N * (half + 1)], biasc[:, half:half + 1], None, ALU.add)
            last.then_inc(bias_ready, 1)
            done(nc.vector.tensor_scalar(g_s[:, 1:2], g_s[:, 0:1], 1.0, None, ALU.add))
            done(nc.vector.reciprocal(g_s[:, 2:3], g_s[:, 1:2]))
            done(nc.vector.tensor_scalar(g_s[:, 3:4], g_s[:, 2:3], -1.0, 1.0, ALU.mult, ALU.add))
            done(nc.vector.tensor_scalar(g_eye[:], eye4, g_s[:, 3:4], None, ALU.mult))

            def arguments(q):
                eng.wait_ge(rt_ready, q + 1)
                done(nc.vector.reciprocal(inv[:], rt[:, QU * q:QU * (q + 1)]))
                done(nc.vector.tensor_tensor(lg[:], raw_l[:, QU * q:QU * (q + 1), :],
                                             over(inv[:].unsqueeze(2), [P, QU, NE]), ALU.mult))
                done(nc.vector.tensor_tensor(lg[:], lg[:], over(base_s[:].unsqueeze(1), [P, QU, NE]), ALU.add))
                groups = QU * NE // NS
                lg4 = lg[:].rearrange("p u (r j) -> p (u r) j", j=NS)
                la4 = la[:].rearrange("p u (r j) -> p (u r) j", j=NS)
                done(nc.vector.tensor_reduce(gmax[:], lg4, AX.X, ALU.max))
                done(nc.vector.tensor_tensor(la4, lg4, over(gmax[:].unsqueeze(2), [P, groups, NS]), ALU.subtract))
                la_h = la[:, :, 0:HH]
                done(nc.vector.tensor_reduce(colmax[:], la_h.rearrange("p u (i j) -> p u j i", j=NS), AX.X, ALU.max))
                done(nc.vector.tensor_tensor(zb[:].rearrange("p i u j -> p u i j"),
                                             la_h.rearrange("p u (i j) -> p u i j", j=NS),
                                             over(colmax[:].unsqueeze(2), [P, QU, NS, NS]), ALU.subtract))
                nc.vector.tensor_scalar(zc[:], zb[:], CLAMP, None, ALU.min).then_inc(args_ready, 1)

            def matrices(q, where):
                at = QU * holds[where].index(q)
                return sk[where][:, :, at:at + QU, :]

            def start(q, where):
                eng.wait_ge(exps_ready, q + 1)
                flat = "p i u j -> p i (u j)"
                m = matrices(q, where)
                sq = soft[:, QU * q:QU * (q + 1), :]
                e4 = e_p[:].rearrange("p u (r j) -> p (u r) j", j=NS)
                row_sum = step(nc.vector.tensor_reduce(s_a[:].rearrange("p i u -> p u i"),
                                                       e_h[:].rearrange("p u (i j) -> p u i j", j=NS), AX.X, ALU.add))
                soft_sum = step(nc.vector.tensor_reduce(s_p[:], e4, AX.X, ALU.add))
                scaled = step(nc.vector.scalar_tensor_tensor(m.rearrange(flat), p_a[:].rearrange(flat), BIG,
                                                             p_b[:].rearrange(flat), ALU.mult, ALU.max))
                need(row_sum)
                row_rec = step(nc.vector.reciprocal(r_a[:], s_a[:]))
                need(soft_sum)
                soft_rec = step(nc.vector.reciprocal(r_p[:], s_p[:]))
                need(max(scaled, row_rec))
                rows = step(nc.vector.tensor_tensor(m, m, over(r_a[:].unsqueeze(3), [P, NS, QU, NS]), ALU.mult))
                need(soft_rec)
                nc.vector.tensor_tensor(sq.rearrange("p u (r j) -> p (u r) j", j=NS), e4,
                                        over(r_p[:].unsqueeze(2), [P, 2 * QU, NS]), ALU.mult).then_inc(soft_ready, 1)
                need(rows)
                col_sum = step(nc.vector.tensor_reduce(s_c[:], m.rearrange("p i u j -> p (u j) i"), AX.X, ALU.add))
                need(col_sum)
                need(step(nc.vector.reciprocal(r_c[:], s_c[:])))
                need(step(nc.vector.scalar_tensor_tensor(m.rearrange(flat), over(r_c[:].unsqueeze(1), [P, NS, NS * QU]),
                                                         BIG, m.rearrange(flat), ALU.mult, ALU.mult)))

            def normalise(at, rows, streams):
                for k in range(3):
                    for n, st in enumerate(streams):
                        if at + k:
                            eng.wait_ge(sink, len(streams) * (at + k - 1) + n + 1)
                        m = sk[st][:]
                        if k == 0:
                            ins = nc.vector.tensor_reduce(sk_s[st][:], m.rearrange("p i u j -> p (i u) j") if rows else
                                                          m.rearrange("p i u j -> p (u j) i"), AX.X, ALU.add)
                        elif k == 1:
                            ins = nc.vector.reciprocal(sk_r[st][:], sk_s[st][:])
                        elif rows:
                            mr = m.rearrange("p i u j -> p (i u) j")
                            ins = nc.vector.scalar_tensor_tensor(mr, over(sk_r[st][:].unsqueeze(2),
                                                                          [P, NS * sk_n[st], NS]),
                                                                 BIG, mr, ALU.mult, ALU.mult)
                        else:
                            mc = m.rearrange("p i u j -> p i (u j)")
                            ins = nc.vector.scalar_tensor_tensor(mc, over(sk_r[st][:].unsqueeze(1),
                                                                          [P, NS, NS * sk_n[st]]),
                                                                 BIG, mc, ALU.mult, ALU.mult)
                        ins.then_inc(sink, 1)

            def settle(n, streams):
                eng.wait_ge(sink, len(streams) * n)
                eng.sem_clear(sink)

            left = [SINK_ITERS - 1] * NQ

            def iterate(streams, n):
                def body(size):
                    for m in range(size):
                        normalise(6 * m, True, streams)
                        normalise(6 * m + 3, False, streams)
                    settle(6 * size, streams)

                for q in set(sum((holds[st] for st in streams), ())):
                    left[q] -= n
                if n >= 2 * ITER_BODY:
                    with eng.Fori(0, n // ITER_BODY) as i:
                        body(ITER_BODY)
                    n = n % ITER_BODY
                if n:
                    body(n)

            def res_to_pe(q, where):
                assert left[q] == 0
                if q:
                    eng.wait_ge(coef_ready, q)
                done(nc.vector.tensor_scalar(hk[:].rearrange("p u (i j) -> p u i j", j=NS),
                                             matrices(q, where).rearrange("p i u j -> p u i j"), 1.0 / BIG, g_s[:, 2:3],
                                             ALU.mult, ALU.mult))
                nc.vector.tensor_tensor(hk[:], hk[:], over(g_eye[:].unsqueeze(1), [P, QU, HH]),
                                        ALU.add).then_inc(hk_ready, 1)

            arguments(0)
            start(0, "0")
            for h, st in enumerate(("0a", "0b")):
                last = nc.vector.tensor_copy(sk[st][:], sk["0"][:, :, 2 * h:2 * h + 2, :])
            done(last)
            iterate(("0a", "0b"), PLAN[0])
            arguments(1)
            iterate(("0a", "0b"), PLAN[1])
            for h, st in enumerate(("0a", "0b")):
                nc.vector.tensor_copy(sk["0"][:, :, 2 * h:2 * h + 2, :], sk[st][:])
            start(1, "1")
            iterate(("0", "1"), PLAN[2])
            arguments(2)
            iterate(("0", "1"), PLAN[3])
            start(2, "2")
            iterate(("0", "1", "2"), AHEAD)
            iterate(("0", "1"), PLAN[4])
            arguments(3)
            iterate(("0", "1"), PLAN[5])
            for q, st in ((0, "01"), (1, "01"), (2, "23")):
                nc.vector.tensor_copy(matrices(q, st), sk[str(q)][:])
            start(3, "23")
            iterate(("01", "23"), left[0])
            res_to_pe(0, "01")
            done(nc.vector.tensor_copy(sk["1"][:], matrices(1, "01")))
            iterate(("1", "23"), left[1])
            res_to_pe(1, "1")
            for q in (2, 3):
                last = nc.vector.tensor_copy(sk[str(q)][:], matrices(q, "23"))
            done(last)
            iterate(("2", "3"), left[2] - PLAN[6])
            eng.sem_inc(sink_near, 1)
            iterate(("2", "3"), left[2])
            res_to_pe(2, "2")
            iterate(("3",), left[3])
            res_to_pe(3, "3")

            def end_out(u, slot):
                for bp in range(2):
                    eng.wait_ge(end_done, 2 * u + bp + 1)
                    pu = part[:, ds(u, 1)].rearrange("p u b c -> p (u b) c")[:, 2 * bp:2 * bp + 2, :]
                    nc.vector.tensor_tensor(pu, mix_ps[slot][bp][:, :].rearrange("p (b c) -> p b c", b=2), pu,
                                            ALU.add).then_inc(end_read, 1)

            eng.wait_ge(x_added, HU)
            for u in range(2):
                end_out(u, u)
            with eng.Fori(1, HU // 2) as i:
                for slot in range(2):
                    end_out(2 * i + slot, slot)


_OUT_SHAPE = (32, 64, 1024)


def kernel(x, cond_128, fside_S_0, L0_cond_weight, L0_cond_c_weight, L0_ffn_W_res, L0_ffn_W_pre, L0_ffn_W_post,
           L0_ffn_H_res_base, L0_ffn_H_pre_base, L0_ffn_H_post_base, L0_ffn_gate, L0_ffn_W_branch):
    import concourse.bacc as _bacc
    from concourse import mybir as _mybir
    from concourse.bass_utils import run_bass_kernel_spmd as _run

    x = np.ascontiguousarray(x)
    cw = np.asarray(L0_cond_weight)
    co_n, gi, taps = cw.shape
    conv_w = np.zeros((3, 32, 2, 3, 32), cw.dtype)
    for half in range(2):
        for g in range(2):
            blk = cw[32 * half + 16 * g:32 * half + 16 * (g + 1)].reshape(16, 16, 3, 3)
            conv_w[:, 16 * g:16 * (g + 1), half, :, 16 * g:16 * (g + 1)] = blk.transpose(3, 1, 2, 0)
    conv_w = conv_w.reshape(96, 2, 3, 32)
    ctx_w = np.ascontiguousarray(np.tile(np.asarray(L0_cond_c_weight).T.reshape(128, 2, 1, 32), (1, 1, 4, 1))
                                 .reshape(128, 2, 128))
    cond_t = np.ascontiguousarray(np.asarray(cond_128).T)
    bias_c = np.ascontiguousarray(np.tile(np.asarray(fside_S_0).reshape(2, 32), (1, 4)).T)
    w_all = np.concatenate([np.asarray(L0_ffn_W_res), np.asarray(L0_ffn_W_pre), np.asarray(L0_ffn_W_post)], axis=0)
    proj_w = np.zeros((128, 2, 4, 32), w_all.dtype)
    proj_w[:, :, :, 0:24] = w_all.reshape(24, 4, 2, 128).transpose(3, 2, 1, 0)
    branch_w = np.ascontiguousarray(np.asarray(L0_ffn_W_branch).reshape(2, 128, 256).transpose(1, 0, 2))
    base = np.concatenate([np.asarray(L0_ffn_H_res_base).reshape(-1), np.asarray(L0_ffn_H_pre_base),
                           np.asarray(L0_ffn_H_post_base)])
    base = np.ascontiguousarray(np.broadcast_to(base[None], (128, 24)))
    gate = np.ascontiguousarray(np.broadcast_to(np.asarray(L0_ffn_gate).reshape(1, 1), (128, 1)))
    consts = np.zeros((128, 128 + 32 + 24 + 16), np.float32)
    consts[:, 0:128] = np.eye(128)
    consts[:, 128:160] = np.tile(np.eye(32), (4, 1))
    consts[:, 160:184] = np.tile(np.eye(32)[:, 0:24], (4, 1))
    consts[:, 184:200] = np.eye(4).reshape(1, 16)

    nc = _bacc.Bacc("TRN2", target_bir_lowering=False, num_devices=1)
    f32 = _mybir.dt.float32
    feeds, args = {}, []
    for name, a in (("x", x), ("conv_w", conv_w), ("ctx_w", ctx_w), ("cond_t", cond_t), ("bias_c", bias_c),
                    ("proj_w", proj_w), ("branch_w", branch_w), ("base", base), ("gate", gate), ("consts", consts)):
        feeds[f"in_{name}"] = a
        args.append(nc.dram_tensor(f"in_{name}", a.shape, f32, kind="ExternalInput").ap())
    out = nc.dram_tensor("out_0", _OUT_SHAPE, f32, kind="ExternalOutput").ap()
    adaln_ffn_program(nc, args[0], out, *args[1:])
    r = _run(nc, [feeds], core_ids=[0])
    return r.results[0]["out_0"]
```
